# Optimizing a Trainium2 kernel written in Bass

```python
import numpy as np
import jax
import jax.numpy as jnp

def _softmax(x, axis=-1):
    return jax.nn.softmax(x, axis=axis)

def _gelu(x):
    return jax.nn.gelu(x, approximate=True)

def _silu(x):
    return jax.nn.silu(x)

def _sigmoid(x):
    return jax.nn.sigmoid(x)

def _layernorm(x, axis=-1, eps=1e-05):
    m = jnp.mean(x, axis=axis, keepdims=True)
    v = jnp.var(x, axis=axis, keepdims=True)
    return (x - m) / jnp.sqrt(v + eps)

def _scatter_add(tgt, idx, src, axis=0):
    return tgt.at[idx].add(src)

def _segment_sum(src, seg, n):
    return jax.ops.segment_sum(src, seg, n)
kernel_name = 'mk_gnn_ffn_d1_gnn_r8_e2c68f'

def setup_inputs(seed: int=0):
    np.random.seed(seed)
    _w = jnp.asarray

    def _rec_inputs():
        import jax
        import jax.numpy as jnp
        _gk = jax.random.key(seed)
        x = -0.0006008 + 1.001 * jax.random.normal(jax.random.fold_in(_gk, 1), (1250, 512), jnp.float32)
        _s = jax.random.randint(jax.random.fold_in(_gk, 2), (10000,), 0, 1250, jnp.int32)
        _d = jax.random.randint(jax.random.fold_in(_gk, 3), (10000,), 0, 1250, jnp.int32)
        _loop = jnp.arange(1250, dtype=jnp.int32)
        src = jnp.concatenate([_s, _d, _loop])
        dst = jnp.concatenate([_d, _s, _loop])
        _o = jnp.argsort(dst, stable=True)
        src = src[_o]
        dst = dst[_o]
        edge_attr_20 = jax.random.uniform(jax.random.fold_in(_gk, 12), (21250, 20), jnp.float32, 0.0, 0.999999)
        edge_attr_3 = -0.0005747 + 0.998114 * jax.random.normal(jax.random.fold_in(_gk, 13), (21250, 3), jnp.float32)
        edge_weight = jax.random.uniform(jax.random.fold_in(_gk, 14), (21250,), jnp.float32, 0.0, 0.999973)
        return (x, src, dst, edge_attr_20, edge_attr_3, edge_weight)
    x, src, dst, edge_attr_20, edge_attr_3, edge_weight = _rec_inputs()

    def _L0_gnn_setup():
        import jax, jax.numpy as jnp
        import numpy as np
        N_ATOMS = 625
        N_EDGES = 6250
        C = 128
        F = 128
        N_RBF = 20
        LOG2 = float(np.log(2.0))
        Y0 = float(1.0 / np.sqrt(4.0 * np.pi))
        Y1_SCALE = float(np.sqrt(3.0 / (4.0 * np.pi)))

        def shifted_softplus(x):
            return jax.nn.softplus(x) - LOG2

        def _forward(x, idx_i, idx_j, f_ij, rcut_ij, r_ij, W_in2f_s, W_in2f_v, Wf1, bf1, Wf2, bf2, W1_s, W1_v, W2_s, W2_v):
            n = x.shape[0]
            e = r_ij.shape[0]
            xs = x[:, :C] @ (W_in2f_s / np.sqrt(C))
            xv = jnp.einsum('nci,cf->nfi', x[:, C:].reshape(n, C, 3), W_in2f_v) / np.sqrt(C)
            sj = xs[idx_j]
            vj = xv[idx_j]
            u = r_ij / jnp.linalg.norm(r_ij, axis=-1, keepdims=True)
            Yv = Y1_SCALE * u
            o0a = sj * Y0
            o0b = jnp.einsum('efi,ei->ef', vj, Yv) / np.sqrt(3.0)
            s2 = jnp.stack([o0a, o0b], axis=-1).reshape(e, 2 * F)
            ova = sj[:, :, None] * Yv[:, None, :]
            ovb = vj * Y0
            v2 = jnp.stack([ova, ovb], axis=2)
            w1 = jnp.cross(vj, Yv[:, None, :]) / np.sqrt(2.0)
            ax, ay, az = (vj[..., 0], vj[..., 1], vj[..., 2])
            bx, by, bz = (Yv[:, None, 0], Yv[:, None, 1], Yv[:, None, 2])
            t = jnp.stack([(ax * by + ay * bx) / np.sqrt(2.0), (ay * bz + az * by) / np.sqrt(2.0), (2.0 * az * bz - ax * bx - ay * by) / np.sqrt(6.0), (az * bx + ax * bz) / np.sqrt(2.0), (ax * bx - ay * by) / np.sqrt(2.0)], axis=-1)
            h = shifted_softplus(f_ij @ Wf1 + bf1)
            W = (h @ Wf2 + bf2) * rcut_ij[:, None]
            m_s = s2 * W[:, :2 * F]
            m_v = (v2.reshape(e, 2 * F, 3) * W[:, 2 * F:4 * F, None]).reshape(e, 6 * F)
            m_w = (w1 * W[:, 4 * F:5 * F, None]).reshape(e, 3 * F)
            m_t = (t * W[:, 5 * F:6 * F, None]).reshape(e, 5 * F)
            x_ij = jnp.concatenate([m_s, m_v, m_w, m_t], axis=1)
            agg = jax.ops.segment_sum(x_ij, idx_i, num_segments=n)
            S = agg[:, :2 * F] @ (W1_s / np.sqrt(2 * F))
            V = jnp.einsum('nmi,mc->nci', agg[:, 2 * F:8 * F].reshape(n, 2 * F, 3), W1_v) / np.sqrt(2 * F)
            S = shifted_softplus(S)
            S = S @ (W2_s / np.sqrt(C))
            V = jnp.einsum('nci,cd->ndi', V, W2_v) / np.sqrt(C)
            return jnp.concatenate([S, V.reshape(n, 3 * C)], axis=1)
        key = jax.random.key(seed)
        ks = jax.random.split(key, 16)
        f32 = jnp.float32
        x = jax.random.normal(ks[0], (N_ATOMS, 4 * C), f32)
        idx_i = jnp.sort(jax.random.randint(ks[1], (N_EDGES,), 0, N_ATOMS))
        idx_j = jax.random.randint(ks[2], (N_EDGES,), 0, N_ATOMS)
        f_ij = jax.random.uniform(ks[3], (N_EDGES, N_RBF), f32)
        rcut_ij = jax.random.uniform(ks[4], (N_EDGES,), f32)
        r_ij = jax.random.normal(ks[5], (N_EDGES, 3), f32)
        W_in2f_s = jax.random.normal(ks[6], (C, F), f32)
        W_in2f_v = jax.random.normal(ks[7], (C, F), f32)
        Wf1 = jax.random.normal(ks[8], (N_RBF, F), f32) / np.sqrt(N_RBF)
        bf1 = 0.1 * jax.random.normal(ks[9], (F,), f32)
        Wf2 = jax.random.normal(ks[10], (F, 6 * F), f32) / np.sqrt(F)
        bf2 = 0.1 * jax.random.normal(ks[11], (6 * F,), f32)
        W1_s = jax.random.normal(ks[12], (2 * F, C), f32)
        W1_v = jax.random.normal(ks[13], (2 * F, C), f32)
        W2_s = jax.random.normal(ks[14], (C, C), f32)
        W2_v = jax.random.normal(ks[15], (C, C), f32)
        return dict(x=x, idx_i=idx_i, idx_j=idx_j, f_ij=f_ij, rcut_ij=rcut_ij, r_ij=r_ij, W_in2f_s=W_in2f_s, W_in2f_v=W_in2f_v, Wf1=Wf1, bf1=bf1, Wf2=Wf2, bf2=bf2, W1_s=W1_s, W1_v=W1_v, W2_s=W2_s, W2_v=W2_v)
    _L0_gnn_all = _L0_gnn_setup()
    _L0_gnn_in = {k: v for k, v in _L0_gnn_all.items() if k in ('W_in2f_s', 'W_in2f_v', 'Wf1', 'bf1', 'Wf2', 'bf2', 'W1_s', 'W1_v', 'W2_s', 'W2_v')}
    del _L0_gnn_all

    def _L0_ffn_setup():
        import jax, jax.numpy as jnp
        import numpy as np
        MIN_EXPERT_CAPACITY = 4
        EPS = 1e-09
        CAPACITY_FACTOR = 2.0

        def cumsum_exclusive(t, axis):
            return jnp.cumsum(t, axis=axis) - t

        def safe_one_hot(idx, depth):
            return jax.nn.one_hot(idx, depth + 1)[..., :depth]

        def top2_gating(x, w_gating):
            b, n, d = x.shape
            e = w_gating.shape[-1]
            raw_gates = jax.nn.softmax(jnp.einsum('bnd,de->bne', x, w_gating), axis=-1)
            gate_1 = jnp.max(raw_gates, axis=-1)
            index_1 = jnp.argmax(raw_gates, axis=-1)
            mask_1 = jax.nn.one_hot(index_1, e, dtype=raw_gates.dtype)
            gates_without_top1 = raw_gates * (1.0 - mask_1)
            gate_2 = jnp.max(gates_without_top1, axis=-1)
            index_2 = jnp.argmax(gates_without_top1, axis=-1)
            mask_2 = jax.nn.one_hot(index_2, e, dtype=raw_gates.dtype)
            denom = gate_1 + gate_2 + EPS
            gate_1 = gate_1 / denom
            gate_2 = gate_2 / denom
            density_1 = jnp.mean(mask_1, axis=-2)
            density_1_proxy = jnp.mean(raw_gates, axis=-2)
            loss = jnp.mean(density_1_proxy * density_1) * float(e * e)
            capacity = max(min(n, int(n * 2 * CAPACITY_FACTOR / e)), MIN_EXPERT_CAPACITY)
            cap_f = float(capacity)
            pos1 = cumsum_exclusive(mask_1, axis=-2) * mask_1
            mask_1 = mask_1 * (pos1 < cap_f).astype(mask_1.dtype)
            mask_1_count = jnp.sum(mask_1, axis=-2, keepdims=True)
            mask_1_flat = jnp.sum(mask_1, axis=-1)
            pos1 = jnp.sum(pos1, axis=-1)
            gate_1 = gate_1 * mask_1_flat
            pos2 = (cumsum_exclusive(mask_2, axis=-2) + mask_1_count) * mask_2
            mask_2 = mask_2 * (pos2 < cap_f).astype(mask_2.dtype)
            mask_2_flat = jnp.sum(mask_2, axis=-1)
            pos2 = jnp.sum(pos2, axis=-1)
            gate_2 = gate_2 * mask_2_flat
            combine = gate_1[..., None, None] * mask_1_flat[..., None, None] * jax.nn.one_hot(index_1, e, dtype=x.dtype)[..., None] * safe_one_hot(pos1.astype(jnp.int32), capacity)[..., None, :] + gate_2[..., None, None] * mask_2_flat[..., None, None] * jax.nn.one_hot(index_2, e, dtype=x.dtype)[..., None] * safe_one_hot(pos2.astype(jnp.int32), capacity)[..., None, :]
            dispatch = (combine > 0).astype(combine.dtype)
            return (dispatch, combine, loss)
        key = jax.random.key(seed)
        k_x, k_g, k_w1, k_w2 = jax.random.split(key, 4)
        b, n, d, e, h = (2, 512, 512, 16, 256)
        x = jax.random.normal(k_x, (b, n, d), dtype=jnp.float32)
        w_gating = jax.random.normal(k_g, (d, e), dtype=jnp.float32) / np.sqrt(d)
        w1 = jax.random.normal(k_w1, (e, d, h), dtype=jnp.float32) / np.sqrt(d)
        w2 = jax.random.normal(k_w2, (e, h, d), dtype=jnp.float32) / np.sqrt(h)
        return {'x': x, 'w_gating': w_gating, 'w1': w1, 'w2': w2}
    _L0_ffn_all = _L0_ffn_setup()
    _L0_ffn_in = {k: v for k, v in _L0_ffn_all.items() if k in ('w_gating', 'w1', 'w2')}
    del _L0_ffn_all
    return {'x': x, 'src': src, 'dst': dst, 'edge_attr_20': edge_attr_20, 'edge_attr_3': edge_attr_3, 'edge_weight': edge_weight, 'L0_gnn_W_in2f_s': _L0_gnn_in['W_in2f_s'], 'L0_gnn_W_in2f_v': _L0_gnn_in['W_in2f_v'], 'L0_gnn_Wf1': _L0_gnn_in['Wf1'], 'L0_gnn_bf1': _L0_gnn_in['bf1'], 'L0_gnn_Wf2': _L0_gnn_in['Wf2'], 'L0_gnn_bf2': _L0_gnn_in['bf2'], 'L0_gnn_W1_s': _L0_gnn_in['W1_s'], 'L0_gnn_W1_v': _L0_gnn_in['W1_v'], 'L0_gnn_W2_s': _L0_gnn_in['W2_s'], 'L0_gnn_W2_v': _L0_gnn_in['W2_v'], 'L0_ffn_w_gating': _L0_ffn_in['w_gating'], 'L0_ffn_w1': _L0_ffn_in['w1'], 'L0_ffn_w2': _L0_ffn_in['w2']}

def reference(x, src, dst, edge_attr_20, edge_attr_3, edge_weight, L0_gnn_W_in2f_s, L0_gnn_W_in2f_v, L0_gnn_Wf1, L0_gnn_bf1, L0_gnn_Wf2, L0_gnn_bf2, L0_gnn_W1_s, L0_gnn_W1_v, L0_gnn_W2_s, L0_gnn_W2_v, L0_ffn_w_gating, L0_ffn_w1, L0_ffn_w2):
    import jax
    import jax.numpy as jnp

    def _L0_gnn_ref(x, idx_i, idx_j, f_ij, rcut_ij, r_ij, W_in2f_s, W_in2f_v, Wf1, bf1, Wf2, bf2, W1_s, W1_v, W2_s, W2_v):
        import jax, jax.numpy as jnp
        import numpy as np
        N_ATOMS = 625
        N_EDGES = 6250
        C = 128
        F = 128
        N_RBF = 20
        LOG2 = float(np.log(2.0))
        Y0 = float(1.0 / np.sqrt(4.0 * np.pi))
        Y1_SCALE = float(np.sqrt(3.0 / (4.0 * np.pi)))

        def shifted_softplus(x):
            return jax.nn.softplus(x) - LOG2

        def _forward(x, idx_i, idx_j, f_ij, rcut_ij, r_ij, W_in2f_s, W_in2f_v, Wf1, bf1, Wf2, bf2, W1_s, W1_v, W2_s, W2_v):
            n = x.shape[0]
            e = r_ij.shape[0]
            xs = x[:, :C] @ (W_in2f_s / np.sqrt(C))
            xv = jnp.einsum('nci,cf->nfi', x[:, C:].reshape(n, C, 3), W_in2f_v) / np.sqrt(C)
            sj = xs[idx_j]
            vj = xv[idx_j]
            u = r_ij / jnp.linalg.norm(r_ij, axis=-1, keepdims=True)
            Yv = Y1_SCALE * u
            o0a = sj * Y0
            o0b = jnp.einsum('efi,ei->ef', vj, Yv) / np.sqrt(3.0)
            s2 = jnp.stack([o0a, o0b], axis=-1).reshape(e, 2 * F)
            ova = sj[:, :, None] * Yv[:, None, :]
            ovb = vj * Y0
            v2 = jnp.stack([ova, ovb], axis=2)
            w1 = jnp.cross(vj, Yv[:, None, :]) / np.sqrt(2.0)
            ax, ay, az = (vj[..., 0], vj[..., 1], vj[..., 2])
            bx, by, bz = (Yv[:, None, 0], Yv[:, None, 1], Yv[:, None, 2])
            t = jnp.stack([(ax * by + ay * bx) / np.sqrt(2.0), (ay * bz + az * by) / np.sqrt(2.0), (2.0 * az * bz - ax * bx - ay * by) / np.sqrt(6.0), (az * bx + ax * bz) / np.sqrt(2.0), (ax * bx - ay * by) / np.sqrt(2.0)], axis=-1)
            h = shifted_softplus(f_ij @ Wf1 + bf1)
            W = (h @ Wf2 + bf2) * rcut_ij[:, None]
            m_s = s2 * W[:, :2 * F]
            m_v = (v2.reshape(e, 2 * F, 3) * W[:, 2 * F:4 * F, None]).reshape(e, 6 * F)
            m_w = (w1 * W[:, 4 * F:5 * F, None]).reshape(e, 3 * F)
            m_t = (t * W[:, 5 * F:6 * F, None]).reshape(e, 5 * F)
            x_ij = jnp.concatenate([m_s, m_v, m_w, m_t], axis=1)
            agg = jax.ops.segment_sum(x_ij, idx_i, num_segments=n)
            S = agg[:, :2 * F] @ (W1_s / np.sqrt(2 * F))
            V = jnp.einsum('nmi,mc->nci', agg[:, 2 * F:8 * F].reshape(n, 2 * F, 3), W1_v) / np.sqrt(2 * F)
            S = shifted_softplus(S)
            S = S @ (W2_s / np.sqrt(C))
            V = jnp.einsum('nci,cd->ndi', V, W2_v) / np.sqrt(C)
            return jnp.concatenate([S, V.reshape(n, 3 * C)], axis=1)
        return _forward(x, idx_i, idx_j, f_ij, rcut_ij, r_ij, W_in2f_s, W_in2f_v, Wf1, bf1, Wf2, bf2, W1_s, W1_v, W2_s, W2_v)

    def _L0_ffn_ref(x, w_gating, w1, w2):
        import jax, jax.numpy as jnp
        import numpy as np
        MIN_EXPERT_CAPACITY = 4
        EPS = 1e-09
        CAPACITY_FACTOR = 2.0

        def cumsum_exclusive(t, axis):
            return jnp.cumsum(t, axis=axis) - t

        def safe_one_hot(idx, depth):
            return jax.nn.one_hot(idx, depth + 1)[..., :depth]

        def top2_gating(x, w_gating):
            b, n, d = x.shape
            e = w_gating.shape[-1]
            raw_gates = jax.nn.softmax(jnp.einsum('bnd,de->bne', x, w_gating), axis=-1)
            gate_1 = jnp.max(raw_gates, axis=-1)
            index_1 = jnp.argmax(raw_gates, axis=-1)
            mask_1 = jax.nn.one_hot(index_1, e, dtype=raw_gates.dtype)
            gates_without_top1 = raw_gates * (1.0 - mask_1)
            gate_2 = jnp.max(gates_without_top1, axis=-1)
            index_2 = jnp.argmax(gates_without_top1, axis=-1)
            mask_2 = jax.nn.one_hot(index_2, e, dtype=raw_gates.dtype)
            denom = gate_1 + gate_2 + EPS
            gate_1 = gate_1 / denom
            gate_2 = gate_2 / denom
            density_1 = jnp.mean(mask_1, axis=-2)
            density_1_proxy = jnp.mean(raw_gates, axis=-2)
            loss = jnp.mean(density_1_proxy * density_1) * float(e * e)
            capacity = max(min(n, int(n * 2 * CAPACITY_FACTOR / e)), MIN_EXPERT_CAPACITY)
            cap_f = float(capacity)
            pos1 = cumsum_exclusive(mask_1, axis=-2) * mask_1
            mask_1 = mask_1 * (pos1 < cap_f).astype(mask_1.dtype)
            mask_1_count = jnp.sum(mask_1, axis=-2, keepdims=True)
            mask_1_flat = jnp.sum(mask_1, axis=-1)
            pos1 = jnp.sum(pos1, axis=-1)
            gate_1 = gate_1 * mask_1_flat
            pos2 = (cumsum_exclusive(mask_2, axis=-2) + mask_1_count) * mask_2
            mask_2 = mask_2 * (pos2 < cap_f).astype(mask_2.dtype)
            mask_2_flat = jnp.sum(mask_2, axis=-1)
            pos2 = jnp.sum(pos2, axis=-1)
            gate_2 = gate_2 * mask_2_flat
            combine = gate_1[..., None, None] * mask_1_flat[..., None, None] * jax.nn.one_hot(index_1, e, dtype=x.dtype)[..., None] * safe_one_hot(pos1.astype(jnp.int32), capacity)[..., None, :] + gate_2[..., None, None] * mask_2_flat[..., None, None] * jax.nn.one_hot(index_2, e, dtype=x.dtype)[..., None] * safe_one_hot(pos2.astype(jnp.int32), capacity)[..., None, :]
            dispatch = (combine > 0).astype(combine.dtype)
            return (dispatch, combine, loss)
        dispatch, combine, loss = top2_gating(x, w_gating)
        expert_inputs = jnp.einsum('bnd,bnec->ebcd', x, dispatch)
        hidden = jax.nn.relu(jnp.einsum('ebcd,edh->ebch', expert_inputs, w1))
        expert_outputs = jnp.einsum('ebch,ehd->ebcd', hidden, w2)
        output = jnp.einsum('ebcd,bnec->bnd', expert_outputs, combine)
        return output
    x = x + _L0_gnn_ref(_layernorm(x, axis=-1), src, dst, edge_attr_20, edge_weight, edge_attr_3, L0_gnn_W_in2f_s, L0_gnn_W_in2f_v, L0_gnn_Wf1, L0_gnn_bf1, L0_gnn_Wf2, L0_gnn_bf2, L0_gnn_W1_s, L0_gnn_W1_v, L0_gnn_W2_s, L0_gnn_W2_v)
    x = x + _L0_ffn_ref(_layernorm(x, axis=-1)[None], L0_ffn_w_gating, L0_ffn_w1, L0_ffn_w2)[0]
    return x

_drawn_inputs = setup_inputs


def setup_inputs(seed=0):
    import zlib

    import numpy as np

    out = dict(_drawn_inputs(seed))
    spreads = {}
    factors = {}
    for name, (base, spread) in spreads.items():
        noise = np.random.default_rng([zlib.crc32(name.encode()), seed]).standard_normal(out[name].shape)
        drawn = base * np.exp(spread * noise) if base else spread * noise
        out[name] = jnp.asarray(drawn.astype(out[name].dtype))
    for name, factor in factors.items():
        out[name] = (out[name] * factor).astype(out[name].dtype)
    return out
```

```python
import concourse.bass as bass
from concourse import mybir
from contextlib import ExitStack
import numpy as np

F32 = mybir.dt.float32
BF16 = mybir.dt.bfloat16
I32 = mybir.dt.int32
U32 = mybir.dt.uint32
ALU = mybir.AluOpType
ACT = mybir.ActivationFunctionType
AX = mybir.AxisListType

N = 1250
E = 21250
D = 512
C = 128
NRBF = 20
P = 125
NC = N // P
EC = E // P
HALF = 4
PAIRS = (E + NC * 255) // 256
TILES = 2 * PAIRS
HALVES = TILES // HALF
PEEL = 6
LOOPS = (HALVES - PEEL) // 4
SLOTCOLS = (HALVES + 2) * HALF
REC = 26
R_W, R_U, R_DST, R_SRC = 20, 21, 24, 25
KS = 5
KS_ACT = 3
STEPS = EC // KS
NE = 16
CAP = min(N, N * 4 // NE)
SJ = 3
SP = CAP // SJ
HID = 256
LN2 = float(np.log(2.0))
EPS = 1e-5
Y0 = float(1.0 / np.sqrt(4.0 * np.pi))
Y1 = float(np.sqrt(3.0 / (4.0 * np.pi)))

assert TILES % HALF == 0 and (HALVES - PEEL) % 4 == 0 and STEPS % 2 == 0 and CAP % SJ == 0 and TILES < 256 and EC < 256


def wait_if(eng, sem, value):
    if isinstance(value, int) and value <= 0:
        return
    eng.wait_ge(sem, value)


def wait_apart(eng, sem, value, tick):
    if isinstance(value, int):
        wait_if(eng, sem, value)
    else:
        eng.wait_ge(sem, value)
        eng.sem_inc(tick)


def build(nc, x_in, src_in, dst_in, ea_in, ev_in, ew_in, win_s, win_v, wf1_in, bf1_in, wf2_in, bf2_in,
          w1s_in, w1v_in, w2s_in, w2v_in, wg_in, we1_in, we2_in, out):
    ctx = ExitStack()
    with ctx:
        def sb(name, shape, dt=F32):
            return ctx.enter_context(nc.sbuf_tensor(name, shape, dt))

        def sem(name):
            return ctx.enter_context(nc.semaphore(name))

        def carve(flat):
            used = [0]

            def piece(parts, shape, dt=F32):
                n = int(np.prod(shape))
                words = n if dt != BF16 else n // 2
                ap = flat[0:parts, used[0]:used[0] + words]
                used[0] += words
                assert used[0] <= flat.shape[1] and words * (1 if dt != BF16 else 2) == n
                if dt != F32:
                    ap = ap.bitcast(dt)
                names = "abcdef"[:len(shape)]
                if len(shape) > 1:
                    ap = ap.rearrange(f"p ({' '.join(names)}) -> p {' '.join(names)}",
                                      **dict(zip(names, shape)))
                return ap
            return piece

        node_tab = nc.dram_tensor("node_tab", [N, D], F32).ap()
        edge_tab = nc.dram_tensor("edge_tab", [E, REC], F32).ap()
        y_tab = nc.dram_tensor("y_tab", [N, D], F32).ap()
        expert_tab = nc.dram_tensor("expert_tab", [NE * CAP, D], F32).ap()

        iota_i = sb("iota_i", [128, 256], I32)
        iota_f = sb("iota_f", [128, 256])
        edge_i = sb("edge_i", [P, EC], I32)
        edge_1 = sb("edge_1", [P, EC])
        part_i = sb("part_i", [128, 1], I32)
        part_f = sb("part_f", [128, 1])
        ident = sb("ident", [128, 128])
        tri = sb("tri", [P, P])
        ones = sb("ones", [P, P])
        ones3 = sb("ones3", [3, 128], BF16)
        win_s_sb = sb("win_s_sb", [C, C])
        win_v_sb = sb("win_v_sb", [C, C])
        wf1 = sb("wf1", [NRBF, C])
        bf1 = sb("bf1", [C, 1])
        wf2_raw = sb("wf2_raw", [C, 4 * C])
        wf2 = sb("wf2", [C, 4, C])
        bf2_raw = sb("bf2_raw", [3, 4 * C])
        bf2_rest = sb("bf2_rest", [3, 4 * C])
        bf2_parts = sb("bf2_parts", [3, 3, 4 * C], BF16)
        bf2_split = sb("bf2_split", [3, 4, C], BF16)
        w1_raw = sb("w1_raw", [C, 2, 2, C])
        w1 = sb("w1", [C, 2, 2, C])
        w2_raw = sb("w2_raw", [C, 2, C])
        w2 = sb("w2", [C, 2, C])
        wg = sb("wg", [C, 4, NE])
        we1 = sb("we1", [128, 2, 4, HID])
        we2 = sb("we2", [128, 2, 2, D])
        x = sb("x", [P, NC, D])
        stats = sb("stats", [P, NC, 6])
        ln_t = sb("ln_t", [P, 6, NC])
        rstd = sb("rstd", [P, NC])
        shift = sb("shift", [P, NC])
        xn = sb("xn", [P, 2, D])
        xT = sb("xT", [128, 2, 4 * P])
        tab_sb = sb("tab_sb", [P, 2, D])
        region = sb("region", [128, NC * 8 * C])
        agg = region[0:P, :].rearrange("p (c m) -> p c m", c=NC)
        o = 0
        ea = region[0:P, o:o + EC * NRBF].rearrange("p (k f) -> p k f", f=NRBF)
        o += EC * NRBF
        ge = region[0:P, o:o + (NC + 1) * EC].rearrange("p (b k) -> p b k", b=NC + 1)
        o += (NC + 1) * EC
        ind_flat = region[0:P, o:o + NC * EC]
        ind = ind_flat.rearrange("p (b k) -> p b k", b=NC)
        o += NC * EC
        incl_flat = region[0:P, o:o + NC * EC]
        incl = incl_flat.rearrange("p (b k) -> p b k", b=NC)
        assert o + NC * EC <= NC * 8 * C
        ev = sb("ev", [P, EC, 3])
        ew = sb("ew", [P, EC])
        src_i = sb("src_i", [P, EC], I32)
        dst_i = sb("dst_i", [P, EC], I32)
        srcf = sb("srcf", [P, EC])
        chunkf = sb("chunkf", [P, EC])
        lane_f = sb("lane_f", [P, EC])
        lane_neg = sb("lane_neg", [P, EC])
        tile_f = sb("tile_f", [P, EC])
        cnt = sb("cnt", [P, 8, NC])
        cnt_i = sb("cnt_i", [P, NC], I32)
        thr = sb("thr", [P, NC + 1])
        shared = sb("shared", [128, EC * (REC + 4 + 3) + KS * (2 * 128 + 2 * TILES) + 2 * KS_ACT * 128])
        early = carve(shared)
        rec_all = early(P, [EC, REC])
        nrm = early(P, [4, EC])
        slot_i = early(P, [3, EC], I32)
        lane_oh = early(P, [2, KS, 128])
        lane_abs = early(P, [2, KS_ACT, 128])
        tile_oh = early(P, [2, KS, TILES])
        idx_all = sb("idx_all", [128, SLOTCOLS], U32)
        valid = sb("valid", [128, SLOTCOLS])
        pair_ge = sb("pair_ge", [1, PAIRS, NC])
        pair_f = sb("pair_f", [1, 2, PAIRS])
        pair_chunk = sb("pair_chunk", [1, PAIRS], I32)
        idx4 = sb("idx4", [128, 2, HALF], U32)
        rec = sb("rec", [128, 4, HALF, REC])
        rec_u = rec[:].bitcast(U32)
        rv = sb("rv", [128, 2, HALF])
        onehot = sb("onehot", [128, 8, P])
        loop = carve(shared)
        xg = loop(128, [8, 4, C])
        fT = sb("fT", [NRBF, HALF * 128])
        sp_t = sb("sp_t", [128, 3, 512])
        h = sb("h", [128, 2, 512])
        dot = sb("dot", [128, 3, C])
        msg = loop(128, [4, 9, C])
        chunks = carve(shared)
        aggc = chunks(P, [2, 8, C])
        aT = chunks(C, [2, 8, P])
        sT = sb("sT", [C, 3, P])
        spT = sb("spT", [C, 2, P])
        vT = sb("vT", [C, 2, 3, P])
        late = carve(region)
        g = late(P, [10, NC, NE])
        gs = late(P, [16, NC])
        reset = late(P, [NE, NC])
        totT = late(P, [2, NE, NC])
        preT = late(P, [2, NE, NC])
        elane_oh = late(P, [2, NC, SP], BF16)
        etile_eq = late(P, [2, NC, 3 * NE], BF16)
        etile_oh = late(P, [2, NC, 2, 3 * NE], BF16)
        xdT = late(128, [4, CAP])
        hT = late(128, [2, CAP])
        yg = late(P, [2, 2, D])
        elane = sb("elane", [P, 2, NC])
        etile = sb("etile", [P, 2, NC])
        cp1 = sb("cp1", [P, NC])
        eidx_f = sb("eidx_f", [SP, 2, 3 * NE])
        eidx = sb("eidx", [SP, 3 * (NE + 1)], U32)
        eidx3 = sb("eidx3", [SP, 2, 3], U32)
        cslot = sb("cslot", [P, 2, NC], U32)
        cidx = sb("cidx", [P, 2, 2], U32)
        ot = sb("ot", [P, 2, 2, D])
        rows = carve(shared)
        xd = rows(SP, [2, SJ, D])
        yo = rows(SP, [2, SJ, D])

        ps = ctx.enter_context(nc.psum_tensor("ps", [128, 8, 512], F32))

        s_sp_tick = sem("s_sp_tick")
        s_pool_tick = sem("s_pool_tick")
        s_pool_step = sem("s_pool_step")
        s_xin = sem("s_xin")
        s_srcin = sem("s_srcin")
        s_evin = sem("s_evin")
        s_eain = sem("s_eain")
        s_win = sem("s_win")
        s_winf = sem("s_winf")
        s_pool_const = sem("s_pool_const")
        s_dve = sem("s_dve")
        s_stats = sem("s_stats")
        s_sqrt = sem("s_sqrt")
        s_norm = sem("s_norm")
        s_nrm2 = sem("s_nrm2")
        s_xn = sem("s_xn")
        s_xnT = sem("s_xnT")
        s_xT = sem("s_xT")
        s_tabmm = sem("s_tabmm")
        s_tabsb = sem("s_tabsb")
        s_tabst = [sem(f"s_tabst{b}") for b in range(2)]
        s_wprep = sem("s_wprep")
        s_recf = sem("s_recf")
        s_recv = sem("s_recv")
        s_rect = sem("s_rect")
        s_rowtot = sem("s_rowtot")
        s_cntmm = sem("s_cntmm")
        s_slotoh = sem("s_slotoh")
        s_lane = sem("s_lane")
        s_labs = sem("s_labs")
        s_laneoh = sem("s_laneoh")
        s_invmm = sem("s_invmm")
        s_idx = sem("s_idx")
        s_agg0 = sem("s_agg0")
        s_idx4 = sem("s_idx4")
        s_recin = [sem(f"s_recin{b}") for b in range(4)]
        s_xgin = [sem(f"s_xgin{b}") for b in range(2)]
        s_rv = sem("s_rv")
        s_onehot = sem("s_onehot")
        s_recT = sem("s_recT")
        s_fT = sem("s_fT")
        s_hmm = sem("s_hmm")
        s_hread = sem("s_hread")
        s_act = sem("s_act")
        s_sp = sem("s_sp")
        s_h = sem("s_h")
        s_w = sem("s_w")
        s_sc = sem("s_sc")
        s_dot = sem("s_dot")
        s_dot3 = sem("s_dot3")
        s_msgv = sem("s_msgv")
        s_msga = sem("s_msga")
        s_scat = sem("s_scat")
        s_acc = sem("s_acc")
        s_aggc = sem("s_aggc")
        s_aggT = sem("s_aggT")
        s_aTv = sem("s_aTv")
        s_aTa = sem("s_aTa")
        s_sv = sem("s_sv")
        s_spa = sem("s_spa")
        s_spT = sem("s_spT")
        s_vT = sem("s_vT")
        s_o = sem("s_o")
        s_x1 = sem("s_x1")
        s_yn = sem("s_yn")
        s_ynT = sem("s_ynT")
        s_yT = sem("s_yT")
        s_yst = [sem(f"s_yst{b}") for b in range(2)]
        s_lgmm = sem("s_lgmm")
        s_lg = sem("s_lg")
        s_gmax = sem("s_gmax")
        s_gexp = sem("s_gexp")
        s_masks = sem("s_masks")
        s_cum = sem("s_cum")
        s_eoh = sem("s_eoh")
        s_einv = sem("s_einv")
        s_eidx = sem("s_eidx")
        s_we = [sem(f"s_we{b}") for b in range(2)]
        s_e3 = sem("s_e3")
        s_xdin = [sem(f"s_xdin{b}") for b in range(2)]
        s_xdT = sem("s_xdT")
        s_xdTsb = sem("s_xdTsb")
        s_hid = sem("s_hid")
        s_hT = sem("s_hT")
        s_eo = sem("s_eo")
        s_yoa = sem("s_yoa")
        s_yov = sem("s_yov")
        s_yost = [sem(f"s_yost{b}") for b in range(2)]
        s_ci = sem("s_ci")
        s_ygin = [sem(f"s_ygin{b}") for b in range(2)]
        s_g1 = sem("s_g1")
        s_out = sem("s_out")
        s_outst = [sem(f"s_outst{b}") for b in range(2)]

        block = ctx.enter_context(nc.Block())

        def halves(eng, step, last=None):
            for q in range(PEEL):
                step(q, q % 4, q // 4, q // 2)
            with eng.Fori(0, LOOPS) as i:
                for k in range(PEEL, PEEL + 4):
                    step(4 * i + k, k % 4, i + k // 4, 2 * i + k // 2)

        def twos(eng, count, step):
            for c in range(2):
                step(c, c, 0)
            with eng.Fori(1, count // 2) as i:
                for b in range(2):
                    step(2 * i + b, b, i)

        @block.sync
        def _(sp):
            sp.dma_start(src_i[:], src_in.rearrange("(p k) -> p k", k=EC)).then_inc(s_srcin, 16)
            sp.dma_start(x[:], x_in.rearrange("(c p) d -> p c d", p=P)).then_inc(s_xin, 16)
            sp.dma_start(ev[:], ev_in.rearrange("(p k) i -> p k i", k=EC)).then_inc(s_evin, 16)
            sp.dma_start(ew[:], ew_in.rearrange("(p k) -> p k", k=EC)).then_inc(s_evin, 16)
            sp.dma_start(dst_i[:], dst_in.rearrange("(p k) -> p k", k=EC)).then_inc(s_evin, 16)
            sp.dma_start(wf2_raw[:], wf2_in[:, 0:4 * C]).then_inc(s_win, 16)
            for r in range(3):
                sp.dma_start(bf2_raw[r:r + 1, :], bf2_in[0:4 * C].rearrange("(a n) -> a n", a=1)).then_inc(s_win, 16)
            sp.dma_start(w1_raw[:, 0, :, :], w1s_in.rearrange("(f t) c -> f t c", t=2)).then_inc(s_win, 16)
            sp.dma_start(w1_raw[:, 1, :, :], w1v_in.rearrange("(f t) c -> f t c", t=2)).then_inc(s_win, 16)
            sp.dma_start(w2_raw[:, 0, :], w2s_in).then_inc(s_win, 16)
            sp.dma_start(w2_raw[:, 1, :], w2v_in).then_inc(s_win, 16)
            sp.dma_start(wg[:], wg_in.rearrange("(a f) e -> f a e", f=C)).then_inc(s_win, 16)

            def store_tab(c, b, n):
                wait_apart(sp, s_tabsb, c + 1, s_sp_tick)
                sp.dma_start(node_tab[bass.ds(P * c, P), :], tab_sb[:, b, :]).then_inc(s_tabst[b], 16)
            sp.wait_ge(s_recf, 1)
            sp.wait_ge(s_recv, 1)
            sp.dma_start(edge_tab.rearrange("(p k) r -> p k r", k=EC), rec_all[:]).then_inc(s_rect, 16)
            twos(sp, NC, store_tab)

            def load_expert(e, b):
                sp.dma_start(we1[:, b, :, :].rearrange("p a h -> p (a h)").rearrange("p (a h) -> p a h", a=4),
                             we1_in[bass.ds(e, 1), :, :].rearrange("o (a p) h -> p (o a) h", p=128)).then_inc(s_we[b], 16)
                sp.dma_start(we2[:, b, :, :],
                             we2_in[bass.ds(e, 1), :, :].rearrange("o (a p) d -> p (o a) d", p=128)).then_inc(s_we[b], 16)
            load_expert(0, 0)
            load_expert(1, 1)

            def store_y(c, b, n):
                wait_apart(sp, s_yn, c + 1, s_sp_tick)
                sp.dma_start(y_tab[bass.ds(P * c, P), :], xn[:, b, :]).then_inc(s_yst[b], 16)
            twos(sp, NC, store_y)

            def expert(e, b, n):
                wait_apart(sp, s_yoa, 2 * e + 2, s_sp_tick)
                wait_apart(sp, s_yov, e + 1, s_sp_tick)
                sp.dma_start(expert_tab[bass.ds(CAP * e, CAP), :].rearrange("(j p) d -> p j d", p=SP),
                             yo[:, b, :, :]).then_inc(s_yost[b], 16)

            def expert_and_load(e, b, n):
                expert(e, b, n)
                load_expert(e + 2, b)
            for e in range(2):
                expert_and_load(e, e, 0)
            with sp.Fori(1, NE // 2 - 1) as i:
                for b in range(2):
                    expert_and_load(2 * i + b, b, i)
            for e in range(NE - 2, NE):
                expert(e, e % 2, e // 2)

            def store_out(c, b, n):
                wait_apart(sp, s_out, c + 1, s_sp_tick)
                sp.dma_start(out[bass.ds(P * c, P), :], ot[:, b, 1, :]).then_inc(s_outst[b], 16)
            twos(sp, NC, store_out)
            for b in range(2):
                sp.wait_ge(s_outst[b], 16 * (NC // 2))

        @block.gpsimd
        def _(pool):
            nc.gpsimd.iota(iota_i[:], pattern=[[1, 256]], base=0, channel_multiplier=0).then_inc(s_pool_const, 1)
            nc.gpsimd.iota(edge_i[:], pattern=[[1, EC]], base=1, channel_multiplier=EC).then_inc(s_pool_const, 1)
            nc.gpsimd.iota(part_i[:], pattern=[[1, 1]], base=0, channel_multiplier=1).then_inc(s_pool_const, 1)
            nc.gpsimd.memset(ident[:], 0.0).then_inc(s_pool_const, 1)
            nc.gpsimd.memset(tri[:], 1.0).then_inc(s_pool_const, 1)
            nc.gpsimd.memset(ones[:], 1.0).then_inc(s_pool_const, 1)
            nc.gpsimd.memset(ones3[:], 1.0).then_inc(s_pool_const, 1)
            pool.wait_ge(s_pool_const, 7)
            nc.gpsimd.affine_select(out=ident[:], in_=ident[:], compare_op=ALU.not_equal, fill=1.0, base=0,
                                    pattern=[[-1, 128]], channel_multiplier=1).then_inc(s_pool_const, 1)
            nc.gpsimd.affine_select(out=tri[:], in_=tri[:], compare_op=ALU.is_gt, fill=0.0, base=0,
                                    pattern=[[1, P]], channel_multiplier=-1).then_inc(s_pool_const, 1)

            pc = [0]

            def link(ins):
                pc[0] += 1
                ins.then_inc(s_pool_step, 1)
                pool.wait_ge(s_pool_step, pc[0])

            g_ = nc.gpsimd
            pool.wait_ge(s_win, 16 * 9)
            for part, (first, odd) in enumerate(((0, 0), (2 * C, 0), (0, 1), (2 * C, 1))):
                g_.tensor_copy(wf2[:, part, :], wf2_raw[:, first + odd:first + 2 * C:2])
            link(g_.tensor_copy(bf2_parts[:, 0, :], bf2_raw[:]))
            link(g_.tensor_tensor(bf2_rest[:], bf2_raw[:], bf2_parts[:, 0, :], ALU.subtract))
            link(g_.tensor_copy(bf2_parts[:, 1, :], bf2_rest[:]))
            link(g_.tensor_tensor(bf2_rest[:], bf2_rest[:], bf2_parts[:, 1, :], ALU.subtract))
            link(g_.tensor_copy(bf2_parts[:, 2, :], bf2_rest[:]))
            for j in range(3):
                link(g_.tensor_scalar(bf2_parts[:, j, :], bf2_parts[:, j, :], ident[0:3, j:j + 1], None, ALU.mult))
            for j in (1, 2):
                link(g_.tensor_tensor(bf2_parts[:, 0, :], bf2_parts[:, 0, :], bf2_parts[:, j, :], ALU.add))
            for part, (first, odd) in enumerate(((0, 0), (2 * C, 0), (0, 1), (2 * C, 1))):
                g_.tensor_copy(bf2_split[:, part, :], bf2_parts[:, 0, first + odd:first + 2 * C:2])
            both = 1.0 / np.sqrt(2.0 * C) / np.sqrt(float(C))
            for kind, odd, scale in ((0, 0, Y0), (0, 1, Y1 / np.sqrt(3.0)), (1, 0, Y1), (1, 1, Y0)):
                g_.tensor_scalar(w1[:, kind, odd, :], w1_raw[:, kind, odd, :], float(scale * both), None, ALU.mult)
            link(g_.tensor_scalar(w2[:], w2_raw[:], float(1.0 / np.sqrt(float(C))), None, ALU.mult))
            pool.wait_ge(s_recf, 1)
            pool.wait_ge(s_recv, 1)
            g_.memset(agg, 0.0).then_inc(s_wprep, 1)

            def gather_rec(q, m4, n4, n2):
                b = m4 % 2
                nc.gpsimd.tensor_copy(idx4[:, b, :], idx_all[:, bass.ds(HALF * q, HALF)]).then_inc(s_idx4, 1)
                wait_apart(pool, s_idx4, q + 1, s_pool_tick)
                wait_apart(pool, s_scat, HALF * (q - 3), s_pool_tick)
                for t in range(HALF):
                    nc.gpsimd.indirect_dma_start(
                        rec[:, m4, t, :], None, edge_tab,
                        bass.IndirectOffsetOnAxis(ap=idx4[:, b, t:t + 1], axis=0)).then_inc(s_recin[m4], 16)

            def gather_xg(q, m4, n4, n2):
                wait_apart(pool, s_recin[m4], 64 * (n4 + 1), s_pool_tick)
                for t in range(HALF):
                    slot = HALF * (m4 % 2) + t
                    wait_apart(pool, s_msgv, HALF * (q - 2) + t + 1, s_pool_tick)
                    nc.gpsimd.indirect_dma_start(
                        xg[:, slot, :, :].rearrange("p a c -> p (a c)"), None, node_tab,
                        bass.IndirectOffsetOnAxis(ap=rec_u[:, m4, t, R_DST:R_DST + 1], axis=0)
                    ).then_inc(s_xgin[m4 % 2], 16)

            def weights_of(q, m4, n4, n2):
                wait_apart(pool, s_onehot, HALF * (q - 1), s_pool_tick)
                nc.gpsimd.tensor_tensor(rv[:, m4 % 2, :], rec[:, m4, :, R_W],
                                        valid[:, bass.ds(HALF * q, HALF)], ALU.mult).then_inc(s_rv, 1)

            pool.wait_ge(s_idx, 1)
            pool.wait_ge(s_rect, 16)
            gather_rec(0, 0, 0, 0)
            gather_rec(1, 1, 0, 0)
            for b in range(2):
                pool.wait_ge(s_tabst[b], 16 * (NC // 2))
            gather_xg(0, 0, 0, 0)
            weights_of(0, 0, 0, 0)

            def step(q, m4, n4, n2):
                gather_rec(q + 2, (m4 + 2) % 4, n4 + (m4 + 2) // 4, n2 + 1)
                gather_xg(q + 1, (m4 + 1) % 4, n4 + (m4 + 1) // 4, n2 + (m4 + 1) // 2 - m4 // 2)
                weights_of(q + 1, (m4 + 1) % 4, n4 + (m4 + 1) // 4, n2)
            halves(pool, step)
            pool.wait_ge(s_recin[(HALVES + 1) % 4], 64 * ((HALVES + 1) // 4 + 1))
            pool.wait_ge(s_xgin[HALVES % 2], 64 * (HALVES // 2 + 1))

            pool.wait_ge(s_acc, PAIRS)

            def copy_agg(c, b, n):
                wait_apart(pool, s_aggT, c - 1, s_pool_tick)
                nc.gpsimd.tensor_copy(aggc[:, b, :, :].rearrange("p m c -> p (m c)"),
                                      agg[:, bass.ds(c, 1), :].rearrange("p o m -> p (o m)")).then_inc(s_aggc, 1)
            twos(pool, NC, copy_agg)

            pool.wait_ge(s_eidx, 1)
            for b in range(2):
                pool.wait_ge(s_yst[b], 16 * (NC // 2))

            def gather_tokens(e, b, n):
                wait_apart(pool, s_xdT, 3 * (e - 1), s_pool_tick)
                nc.gpsimd.tensor_copy(eidx3[:, b, :], eidx[:, bass.ds(SJ * e, SJ)]).then_inc(s_e3, 1)
                wait_apart(pool, s_e3, e + 1, s_pool_tick)
                for j in range(SJ):
                    nc.gpsimd.indirect_dma_start(
                        xd[:, b, j, :], None, y_tab,
                        bass.IndirectOffsetOnAxis(ap=eidx3[:, b, j:j + 1], axis=0)).then_inc(s_xdin[b], 16)
            twos(pool, NE, gather_tokens)
            gather_tokens(NE, NE % 2, NE // 2)

            for b in range(2):
                pool.wait_ge(s_yost[b], 16 * (NE // 2))
            pool.wait_ge(s_xdin[NE % 2], 48 * (NE // 2 + 1))

            def gather_results(c, b, n):
                wait_apart(pool, s_out, c - 1, s_pool_tick)
                nc.gpsimd.tensor_copy(cidx[:, b, :].unsqueeze(2), cslot[:, :, bass.ds(c, 1)]).then_inc(s_ci, 1)
                wait_apart(pool, s_ci, c + 1, s_pool_tick)
                for a in range(2):
                    nc.gpsimd.indirect_dma_start(
                        yg[:, b, a, :], None, expert_tab,
                        bass.IndirectOffsetOnAxis(ap=cidx[:, b, a:a + 1], axis=0)).then_inc(s_ygin[b], 16)
            twos(pool, NC, gather_results)

        @block.scalar
        def _(act):
            chain = [0]

            def link(ins):
                chain[0] += 1
                ins.then_inc(s_act, 1)
                act.wait_ge(s_act, chain[0])

            act.dma_start(ea, ea_in.rearrange("(p k) f -> p k f", k=EC)).then_inc(s_eain, 16)
            act.dma_start(win_s_sb[:], win_s).then_inc(s_winf, 16)
            act.dma_start(win_v_sb[:], win_v).then_inc(s_winf, 16)
            act.dma_start(wf1[:], wf1_in).then_inc(s_winf, 16)
            act.dma_start(bf1[:], bf1_in.rearrange("(c a) -> c a", a=1)).then_inc(s_winf, 16)

            act.wait_ge(s_stats, 1)
            nc.scalar.activation(ln_t[:, 3, :], ln_t[:, 2, :], ACT.Sqrt).then_inc(s_sqrt, 1)
            act.wait_ge(s_nrm2, 1)
            nc.scalar.activation(nrm[:, 1, :], nrm[:, 0, :], ACT.Sqrt).then_inc(s_sqrt, 1)
            act.wait_ge(s_eain, 16)
            nc.scalar.copy(rec_all[:, :, 0:NRBF], ea).then_inc(s_recf, 1)

            act.wait_ge(s_norm, 1)

            def norm_x(c, b):
                wait_if(act, s_xnT, c - 1)
                nc.scalar.activation(xn[:, b, :], x[:, bass.ds(c, 1), :].rearrange("p o d -> p (o d)"), ACT.Identity,
                                     bias=shift[:, bass.ds(c, 1)], scale=rstd[:, bass.ds(c, 1)]).then_inc(s_xn, 1)

            def copy_xT(c, b):
                act.wait_ge(s_xnT, c + 1)
                wait_if(act, s_tabmm, c - 1)
                nc.scalar.copy(xT[:, b, :], ps[:, 6 + b, 0:4 * P]).then_inc(s_xT, 1)

            def copy_tab(c, b, n):
                act.wait_ge(s_tabmm, c + 1)
                wait_if(act, s_tabst[b], 16 * n)
                nc.scalar.copy(tab_sb[:, b, :], ps[0:P, 4 + b, :]).then_inc(s_tabsb, 1)

            norm_x(0, 0)
            norm_x(1, 1)
            copy_xT(0, 0)

            def project(c, b, n, normed=True, copied=True):
                if copied:
                    copy_xT(c + 1, 1 - b)
                if normed:
                    norm_x(c + 2, b)
                copy_tab(c, b, n)
            project(0, 0, 0)
            project(1, 1, 0)
            with act.Fori(1, NC // 2 - 1) as i:
                for b in range(2):
                    project(2 * i + b, b, i)
            project(NC - 2, 0, NC // 2 - 1, normed=False)
            project(NC - 1, 1, NC // 2 - 1, normed=False, copied=False)

            act.wait_ge(s_lane, 1)

            def lane_step(s, b, n):
                wait_if(act, s_laneoh, s - 1)
                for k in range(KS_ACT):
                    ins = nc.scalar.activation(lane_abs[:, b, k, :], iota_f[0:P, 0:128], ACT.Abs,
                                               bias=lane_neg[:, bass.ds(KS * s + k, 1)])
                ins.then_inc(s_labs, 1)
                act.wait_ge(s_labs, s + 1)
                wait_if(act, s_invmm, s - 1)
                nc.scalar.activation(lane_oh[:, b, 0:KS_ACT, :], lane_abs[:, b, :, :], ACT.Relu, bias=1.0,
                                     scale=-1.0).then_inc(s_laneoh, 1)
            twos(act, STEPS, lane_step)

            def copy_features(q):
                act.wait_ge(s_recT, q + 1)
                wait_if(act, s_hmm, q)
                nc.scalar.copy(fT[:], ps[0:NRBF, 6, :]).then_inc(s_fT, 1)

            def softplus_exp(q):
                act.wait_ge(s_hmm, q + 1)
                wait_if(act, s_h, q)
                nc.scalar.activation(sp_t[:, 0, :], ps[:, 7, :], ACT.Abs, bias=bf1[:, 0:1]).then_inc(s_act, 1)
                nc.scalar.activation(sp_t[:, 2, :], ps[:, 7, :], ACT.Relu, bias=bf1[:, 0:1]).then_inc(s_hread, 1)
                act.wait_ge(s_act, 2 * q + 1)
                nc.scalar.activation(sp_t[:, 1, :], sp_t[:, 0, :], ACT.Exp, scale=-1.0).then_inc(s_act, 1)

            def softplus_ln(q):
                act.wait_ge(s_act, 2 * q + 2)
                nc.scalar.activation(sp_t[:, 0, :], sp_t[:, 1, :], ACT.Ln, bias=1.0).then_inc(s_sp, 1)

            def scaled(q, m4, t):
                act.wait_ge(s_sc, HALF * q + t + 1)
                for i in range(3):
                    ins = nc.scalar.activation(msg[:, t, 5 + i, :], msg[:, t, 8, :], ACT.Copy,
                                               scale=rec[:, m4, t, R_U + i:R_U + i + 1])
                ins.then_inc(s_msga, 1)

            act.wait_ge(s_winf, 64)
            act.preload_act_table_set("natural_log_exp_and_others")
            copy_features(0)
            softplus_exp(0)
            softplus_ln(0)
            copy_features(1)

            def step(q, m4, n4, n2):
                scaled(q, m4, 0)
                scaled(q, m4, 1)
                softplus_exp(q + 1)
                softplus_ln(q + 1)
                scaled(q, m4, 2)
                copy_features(q + 2)
                scaled(q, m4, 3)
            halves(act, step)
            chain[0] = 2 * (HALVES + 1)

            def chunk(c, b, n):
                act.wait_ge(s_aggT, c + 1)
                wait_if(act, s_sv, c - 1)
                nc.scalar.copy(aT[:, b, 4:8, :], ps[:, 2 * b + 1, 0:4 * P].rearrange("p (m n) -> p m n", m=4)).then_inc(s_aTa, 1)
                act.wait_ge(s_sv, c + 1)
                wait_if(act, s_spT, c)
                nc.scalar.activation(sT[:, 0, :], ps[:, 6 + b, 0:P], ACT.Abs).then_inc(s_act, 1)
                nc.scalar.activation(sT[:, 2, :], ps[:, 6 + b, 0:P], ACT.Relu)
                act.wait_ge(s_act, chain[0] + 2 * c + 1)
                nc.scalar.activation(sT[:, 1, :], sT[:, 0, :], ACT.Exp, scale=-1.0).then_inc(s_act, 1)
                act.wait_ge(s_act, chain[0] + 2 * c + 2)
                nc.scalar.activation(sT[:, 0, :], sT[:, 1, :], ACT.Ln, bias=1.0).then_inc(s_spa, 1)
            twos(act, NC, chunk)
            chain[0] += 2 * NC

            act.wait_ge(s_stats, 2)
            nc.scalar.activation(ln_t[:, 3, :], ln_t[:, 2, :], ACT.Sqrt).then_inc(s_sqrt, 1)
            act.preload_act_table_set("natural_log_exp_and_others")
            act.wait_ge(s_norm, 2)

            def norm(c, b, n):
                wait_if(act, s_ynT, c - 1)
                wait_if(act, s_yst[b], 16 * n)
                nc.scalar.activation(xn[:, b, :], x[:, bass.ds(c, 1), :].rearrange("p o d -> p (o d)"), ACT.Identity,
                                     bias=shift[:, bass.ds(c, 1)], scale=rstd[:, bass.ds(c, 1)]).then_inc(s_yn, 1)
                act.wait_ge(s_ynT, c + 1)
                wait_if(act, s_lgmm, c - 1)
                nc.scalar.copy(xT[:, b, :], ps[:, b, 0:4 * P]).then_inc(s_yT, 1)
            twos(act, NC, norm)

            act.wait_ge(s_gmax, 1)
            nc.scalar.activation(g[:, 1, :, :], g[:, 0, :, :], ACT.Exp).then_inc(s_gexp, 1)

            def expert(e, b, n):
                for a in range(2):
                    act.wait_ge(s_hid, 2 * e + a + 1)
                    if a == 0:
                        wait_if(act, s_eo, 3 * e)
                    nc.scalar.activation(hT[:, a, :], ps[:, 3 + a, 0:CAP], ACT.Relu).then_inc(s_hT, 1)
                wait_if(act, s_yost[b], 16 * n)
                for j in range(2):
                    act.wait_ge(s_eo, 3 * e + j + 1)
                    nc.scalar.copy(yo[:, b, j, :], ps[0:SP, 5 + j, :]).then_inc(s_yoa, 1)
            twos(act, NE, expert)

        @block.vector
        def _(dve):
            chain = [0]

            def link(ins):
                chain[0] += 1
                ins.then_inc(s_dve, 1)
                dve.wait_ge(s_dve, chain[0])

            v = nc.vector

            dve.wait_ge(s_pool_const, 3)
            v.tensor_copy(edge_1[:], edge_i[:])
            v.tensor_scalar(thr[:], iota_i[0:P, 0:NC + 1], float(P), None, ALU.mult)
            v.memset(idx_all[:, TILES:SLOTCOLS], 0)
            v.memset(valid[:, TILES:SLOTCOLS], 0.0)
            v.memset(eidx[:, 3 * NE:3 * NE + 3], 0)
            link(v.tensor_copy(part_f[:], part_i[:]))
            link(v.tensor_copy(iota_f[:], iota_i[:]))

            def norm_scales(which):
                me, mo = stats[:, :, 1], stats[:, :, 4]
                link(v.tensor_tensor(ln_t[:, 0, :], me, mo, ALU.add))
                link(v.tensor_tensor(ln_t[:, 1, :], me, mo, ALU.subtract))
                link(v.tensor_tensor(ln_t[:, 2, :], stats[:, :, 2], stats[:, :, 5], ALU.add))
                link(v.tensor_scalar(ln_t[:, 4, :], ln_t[:, 1, :], 0.5, None, ALU.mult))
                link(v.tensor_tensor(ln_t[:, 5, :], ln_t[:, 4, :], ln_t[:, 4, :], ALU.mult))
                link(v.tensor_scalar(ln_t[:, 4, :], ln_t[:, 2, :], 1.0 / D, EPS, ALU.mult, ALU.add))
                v.tensor_tensor(ln_t[:, 2, :], ln_t[:, 4, :], ln_t[:, 5, :], ALU.add).then_inc(s_stats, 1)

            def norm_finish(which):
                link(v.reciprocal(ln_t[:, 4, :], ln_t[:, 3, :]))
                link(v.tensor_tensor(ln_t[:, 5, :], ln_t[:, 2, :], ln_t[:, 4, :], ALU.mult))
                link(v.tensor_tensor(ln_t[:, 4, :], ln_t[:, 5, :], ln_t[:, 3, :], ALU.add))
                link(v.tensor_scalar(ln_t[:, 5, :], ln_t[:, 4, :], 0.5, None, ALU.mult))
                link(v.reciprocal(rstd[:], ln_t[:, 5, :]))
                v.scalar_tensor_tensor(shift[:], ln_t[:, 0, :], -0.5, rstd[:], ALU.mult, ALU.mult).then_inc(s_norm, 1)

            dve.wait_ge(s_srcin, 16)
            link(v.tensor_copy(srcf[:], src_i[:]))
            link(v.tensor_tensor(ge, srcf[:].unsqueeze(1).broadcast_to([P, NC + 1, EC]),
                                 thr[:].unsqueeze(2).broadcast_to([P, NC + 1, EC]), ALU.is_ge))
            link(v.tensor_tensor(ind, ge[:, 0:NC, :], ge[:, 1:NC + 1, :], ALU.subtract))
            v.tensor_reduce(cnt[:, 0, :], ind, AX.X, ALU.add).then_inc(s_rowtot, 1)

            dve.wait_ge(s_xin, 16)
            with dve.Fori(0, NC) as c:
                v.bn_stats(stats[:, bass.ds(c, 1), :].rearrange("p o s -> p (o s)"),
                           x[:, bass.ds(c, 1), :].rearrange("p o d -> p (o d)")).then_inc(s_dve, 1)
            chain[0] += NC
            dve.wait_ge(s_dve, chain[0])
            norm_scales(0)
            dve.wait_ge(s_evin, 48)
            link(v.tensor_tensor(nrm[:, 1:4, :].rearrange("p i k -> p k i"), ev[:], ev[:], ALU.mult))
            v.tensor_reduce(nrm[:, 0, :], nrm[:, 1:4, :].rearrange("p i k -> p k i"), AX.X, ALU.add).then_inc(s_nrm2, 1)
            dve.wait_ge(s_sqrt, 1)
            norm_finish(0)

            reset_flat = region[0:P, EC * NRBF:EC * NRBF + NC * EC]
            link(v.memset(reset_flat, 1.0))
            link(v.memset(reset_flat.rearrange("p (b k) -> p b k", b=NC)[:, :, 0:1], 0.0))
            link(v.tensor_tensor_scan(incl_flat, reset_flat, ind_flat, 0.0, ALU.mult, ALU.add))
            dve.wait_ge(s_cntmm, 1)
            link(v.tensor_scalar(cnt_i[:], ps[0:P, 0, 16:16 + NC], 255.0, None, ALU.add))
            link(v.tensor_scalar(cnt_i[:], cnt_i[:], 8, None, ALU.arith_shift_right))
            link(v.tensor_copy(cnt[:, 1, :], cnt_i[:]))
            link(v.memset(cnt[:, 6, :], 1.0))
            link(v.tensor_tensor_scan(cnt[:, 2, :], cnt[:, 6, :], cnt[:, 1, :], 0.0, ALU.mult, ALU.add))
            link(v.tensor_tensor(cnt[:, 3, :], cnt[:, 2, :], cnt[:, 1, :], ALU.subtract))
            link(v.tensor_scalar(cnt[:, 4, :], cnt[:, 3, :], 256.0, -1.0, ALU.mult, ALU.add))
            link(v.tensor_tensor(cnt[:, 5, :], cnt[:, 4, :], ps[0:P, 0, 0:NC], ALU.add))
            link(v.tensor_tensor(incl, incl, cnt[:, 5, :].unsqueeze(2).broadcast_to([P, NC, EC]), ALU.add))
            link(v.tensor_tensor(incl, incl, ind, ALU.mult))
            link(v.tensor_reduce(chunkf[:], incl.rearrange("p b k -> p k b"), AX.X, ALU.add))
            link(v.tensor_copy(slot_i[:, 0, :], chunkf[:]))
            link(v.tensor_scalar(slot_i[:, 1, :], slot_i[:, 0, :], 7, None, ALU.arith_shift_right))
            link(v.tensor_scalar(slot_i[:, 2, :], slot_i[:, 0, :], 127, None, ALU.bitwise_and))
            link(v.tensor_copy(tile_f[:], slot_i[:, 1, :]))
            link(v.tensor_copy(lane_f[:], slot_i[:, 2, :]))
            v.tensor_scalar(lane_neg[:], lane_f[:], -1.0, None, ALU.mult).then_inc(s_lane, 1)

            link(v.tensor_tensor(incl, ind, thr[:, 0:NC].unsqueeze(2).broadcast_to([P, NC, EC]), ALU.mult))
            link(v.tensor_reduce(chunkf[:], incl.rearrange("p b k -> p k b"), AX.X, ALU.add))
            v.tensor_tensor(rec_all[:, :, R_SRC], srcf[:], chunkf[:], ALU.subtract)
            v.tensor_copy(rec_all[:, :, R_W], ew[:])
            v.tensor_copy(rec_all[:, :, R_DST].bitcast(I32), dst_i[:])
            dve.wait_ge(s_sqrt, 2)
            link(v.reciprocal(nrm[:, 2, :], nrm[:, 1, :]))
            link(v.tensor_tensor(nrm[:, 3, :], nrm[:, 0, :], nrm[:, 2, :], ALU.mult))
            link(v.tensor_tensor(nrm[:, 2, :], nrm[:, 3, :], nrm[:, 1, :], ALU.add))
            link(v.tensor_scalar(nrm[:, 3, :], nrm[:, 2, :], 0.5, None, ALU.mult))
            link(v.reciprocal(nrm[:, 1, :], nrm[:, 3, :]))
            v.tensor_tensor(rec_all[:, :, R_U:R_U + 3], ev[:], nrm[:, 1, :].unsqueeze(2).broadcast_to([P, EC, 3]),
                            ALU.mult).then_inc(s_recv, 1)

            def tile_step(s, b, n):
                wait_if(dve, s_invmm, s - 1)
                for k in range(KS):
                    col = KS * s + k
                    if k >= KS_ACT:
                        v.tensor_scalar(lane_oh[:, b, k, :], iota_f[0:P, 0:128], lane_f[:, bass.ds(col, 1)], None,
                                        ALU.is_equal)
                    ins = v.tensor_scalar(tile_oh[:, b, k, :], iota_f[0:P, 0:TILES], tile_f[:, bass.ds(col, 1)],
                                          edge_1[:, bass.ds(col, 1)], ALU.is_equal, ALU.mult)
                ins.then_inc(s_slotoh, 1)
            twos(dve, STEPS, tile_step)

            dve.wait_ge(s_invmm, STEPS)
            link(v.tensor_scalar(idx_all[:, 0:TILES], ps[:, 1, 0:TILES], -1.0, 0.0, ALU.add, ALU.max))
            v.tensor_scalar(valid[:, 0:TILES], ps[:, 1, 0:TILES], 1.0, None, ALU.min).then_inc(s_idx, 1)
            link(v.tensor_tensor(pair_ge[:], cnt[0:1, 2, :].unsqueeze(1).broadcast_to([1, PAIRS, NC]),
                                 iota_f[0:1, 0:PAIRS].unsqueeze(2).broadcast_to([1, PAIRS, NC]), ALU.is_le))
            link(v.tensor_reduce(pair_f[:, 0, :], pair_ge[:], AX.X, ALU.add))
            link(v.tensor_scalar(pair_chunk[:], pair_f[:, 0, :], float(NC - 1), None, ALU.min))

            def make_h(q, b):
                dve.wait_ge(s_sp, q + 1)
                wait_if(dve, s_w, HALF * (q - 1))
                v.scalar_tensor_tensor(h[:, b, :], sp_t[:, 2, :], -LN2, sp_t[:, 0, :], ALU.add, ALU.add).then_inc(s_h, 1)

            def messages(q, m4, n2, t):
                T = HALF * q + t
                slot = HALF * (m4 % 2) + t
                xs = xg[:, slot, :, :]
                u = rec[:, m4, t, :]
                W = ps[:, t % 2, :].rearrange("p (g c) -> p g c", g=4)
                m = msg[:, t, :, :]
                if t == 0:
                    dve.wait_ge(s_xgin[m4 % 2], 64 * (n2 + 1))
                v.tensor_scalar(dot[:, 0, :], xs[:, 1, :], u[:, R_U:R_U + 1], None, ALU.mult).then_inc(s_dot, 1)
                dve.wait_ge(s_w, T + 1)
                wait_if(dve, s_scat, T - 3)
                v.tensor_tensor(m[:, 0:9:8, :], W[:, 0:2, :], xs[:, 0:1, :].broadcast_to([128, 2, C]),
                                ALU.mult).then_inc(s_sc, 1)
                dve.wait_ge(s_dot, 2 * T + 1)
                v.scalar_tensor_tensor(dot[:, 1, :], xs[:, 2, :], u[:, R_U + 1:R_U + 2], dot[:, 0, :],
                                       ALU.mult, ALU.add).then_inc(s_dot, 1)
                v.tensor_tensor(m[:, 1:4, :], W[:, 3:4, :].broadcast_to([128, 3, C]), xs[:, 1:4, :], ALU.mult)
                dve.wait_ge(s_dot, 2 * T + 2)
                link3 = v.scalar_tensor_tensor(dot[:, 2, :], xs[:, 3, :], u[:, R_U + 2:R_U + 3], dot[:, 1, :],
                                               ALU.mult, ALU.add)
                link3.then_inc(s_dot3, 1)
                dve.wait_ge(s_dot3, T + 1)
                v.tensor_tensor(m[:, 4, :], W[:, 2, :], dot[:, 2, :], ALU.mult).then_inc(s_msgv, 1)

            def accumulate(j, b):
                chunk = dve.value_load(pair_chunk[0:1, bass.ds(j, 1)], min_val=0, max_val=NC - 1)
                dve.wait_ge(s_scat, 2 * j + 2)
                wait_if(dve, s_acc, j)
                to = agg[:, bass.ds(chunk, 1), :].rearrange("p o m -> p (o m)")
                v.tensor_tensor(to, to, ps[0:P, 2 + 2 * b:4 + 2 * b, :].rearrange("p a m -> p (a m)"),
                                ALU.add).then_inc(s_acc, 1)

            def one_hot(q, m4, t):
                slot = HALF * (m4 % 2) + t
                if t == 0:
                    dve.wait_ge(s_rv, q + 1)
                wait_if(dve, s_scat, HALF * (q - 2) + t + 1)
                v.tensor_scalar(onehot[:, slot, :], iota_f[:, 0:P], rec[:, m4, t, R_SRC:R_SRC + 1],
                                rv[:, m4 % 2, t:t + 1], ALU.is_equal, ALU.mult).then_inc(s_onehot, 1)

            for t in range(HALF):
                one_hot(0, 0, t)
            make_h(0, 0)

            def step(q, m4, n4, n2):
                after = (m4 + 1) % 4
                messages(q, m4, n2, 0)
                one_hot(q + 1, after, 0)
                messages(q, m4, n2, 1)
                one_hot(q + 1, after, 1)
                if not (isinstance(q, int) and q == 0):
                    accumulate(2 * q - 1, 1)
                messages(q, m4, n2, 2)
                one_hot(q + 1, after, 2)
                make_h(q + 1, after % 2)
                messages(q, m4, n2, 3)
                one_hot(q + 1, after, 3)
                accumulate(2 * q, 0)
            halves(dve, step)
            accumulate(PAIRS - 1, 1)

            def chunk(c, b, n):
                dve.wait_ge(s_aggT, c + 1)
                wait_if(dve, s_sv, c - 1)
                v.tensor_copy(aT[:, b, 0:4, :], ps[:, 2 * b, 0:4 * P].rearrange("p (m n) -> p m n", m=4)).then_inc(s_aTv, 1)
                dve.wait_ge(s_sv, c + 1)
                wait_if(dve, s_o, c - 1)
                v.tensor_copy(vT[:, b, :, :], ps[:, 4 + b, P:4 * P].rearrange("p (i n) -> p i n", i=3)).then_inc(s_vT, 1)
                dve.wait_ge(s_spa, c + 1)
                v.scalar_tensor_tensor(spT[:, b, :], sT[:, 2, :], -LN2, sT[:, 0, :], ALU.add, ALU.add).then_inc(s_spT, 1)
                dve.wait_ge(s_o, c + 1)
                xc = x[:, bass.ds(c, 1), :].rearrange("p o d -> p (o d)")
                v.tensor_tensor(xc[:, 0:C], xc[:, 0:C], ps[0:P, 6 + b, 0:C], ALU.add)
                xv = xc[:, C:D].rearrange("p (d i) -> p i d", i=3)
                v.tensor_tensor(xv, xv, ps[0:P, 6 + b, C:D].rearrange("p (i d) -> p i d", i=3), ALU.add).then_inc(s_x1, 1)
                dve.wait_ge(s_x1, c + 1)
                v.bn_stats(stats[:, bass.ds(c, 1), :].rearrange("p o s -> p (o s)"), xc).then_inc(s_dve, 1)
            twos(dve, NC, chunk)
            chain[0] += NC
            dve.wait_ge(s_dve, chain[0])
            norm_scales(1)
            dve.wait_ge(s_sqrt, 3)
            norm_finish(1)

            def logits(c, b, n):
                dve.wait_ge(s_lgmm, c + 1)
                v.tensor_copy(g[:, 2, bass.ds(c, 1), :].rearrange("p o e -> p (o e)"), ps[0:P, 2 + b, 0:NE]).then_inc(s_lg, 1)
            twos(dve, NC, logits)
            dve.wait_ge(s_lg, NC)

            def by_expert(a):
                return a.unsqueeze(2).broadcast_to([P, NC, NE])
            iota_e = iota_f[0:P, 0:NE].unsqueeze(1).broadcast_to([P, NC, NE])
            link(v.tensor_reduce(gs[:, 0, :], g[:, 2, :, :], AX.X, ALU.max))
            link(v.tensor_tensor(g[:, 0, :, :], g[:, 2, :, :], by_expert(gs[:, 0, :]), ALU.subtract))
            v.engine_nop().then_inc(s_gmax, 1)
            dve.wait_ge(s_gexp, 1)
            link(v.tensor_reduce(gs[:, 0, :], g[:, 1, :, :], AX.X, ALU.add))
            link(v.reciprocal(gs[:, 1, :], gs[:, 0, :]))
            link(v.tensor_tensor(g[:, 0, :, :], g[:, 1, :, :], by_expert(gs[:, 1, :]), ALU.mult))
            for a in range(2):
                raw = g[:, 0, :, :]
                link(v.tensor_reduce(gs[:, 2 + a, :], raw, AX.X, ALU.max))
                link(v.tensor_tensor(g[:, 1, :, :], raw, by_expert(gs[:, 2 + a, :]), ALU.is_equal))
                link(v.tensor_scalar(g[:, 2, :, :], g[:, 1, :, :], -float(NE), float(NE), ALU.mult, ALU.add))
                link(v.tensor_tensor(g[:, 1, :, :], g[:, 2, :, :], iota_e, ALU.add))
                link(v.tensor_reduce(gs[:, 4 + a, :], g[:, 1, :, :], AX.X, ALU.min))
                link(v.tensor_tensor(g[:, 4 + a, :, :], iota_e, by_expert(gs[:, 4 + a, :]), ALU.is_equal))
                if a == 0:
                    link(v.tensor_tensor(g[:, 1, :, :], raw, g[:, 4, :, :], ALU.mult))
                    link(v.tensor_tensor(raw, raw, g[:, 1, :, :], ALU.subtract))
            v.engine_nop().then_inc(s_masks, 1)
            link(v.tensor_tensor(gs[:, 6, :], gs[:, 2, :], gs[:, 3, :], ALU.add))
            link(v.tensor_scalar(gs[:, 6, :], gs[:, 6, :], 1e-9, None, ALU.add))
            link(v.reciprocal(gs[:, 7, :], gs[:, 6, :]))
            link(v.tensor_tensor(gs[:, 2:4, :], gs[:, 2:4, :], gs[:, 7:8, :].broadcast_to([P, 2, NC]), ALU.mult))

            link(v.memset(reset[:], 1.0))
            link(v.memset(reset[:, :, 0:1], 0.0))
            dve.wait_ge(s_cum, 1)
            for a in range(2):
                tot = ps[0:P, 5, 160 * a:160 * a + 160].rearrange("p (c e) -> p e c", c=NC)
                link(v.tensor_copy(totT[:, a, :, :], tot))
                link(v.tensor_tensor_scan(preT[:, a, :, :].rearrange("p e c -> p (e c)"),
                                          reset[:].rearrange("p e c -> p (e c)"),
                                          totT[:, a, :, :].rearrange("p e c -> p (e c)"), 0.0, ALU.mult, ALU.add))
            link(v.tensor_tensor(totT[:], preT[:], totT[:], ALU.subtract))
            link(v.tensor_scalar(reset[:, :, 0:1], preT[:, 0, :, NC - 1:NC], float(CAP), None, ALU.min))
            link(v.tensor_tensor(totT[:, 1, :, :], totT[:, 1, :, :], reset[:, :, 0:1].broadcast_to([P, NE, NC]), ALU.add))
            for a in range(2):
                cum = ps[0:P, 4, 160 * a:160 * a + 160].rearrange("p (c e) -> p c e", c=NC)
                link(v.tensor_tensor(g[:, 6 + a, :, :], cum, totT[:, a, :, :].rearrange("p e c -> p c e"), ALU.add))
                link(v.tensor_tensor(g[:, 8 + a, :, :], g[:, 6 + a, :, :], g[:, 4 + a, :, :], ALU.mult))
                link(v.tensor_reduce(gs[:, 8 + a, :], g[:, 8 + a, :, :], AX.X, ALU.add))
            pos, fits, gate, expert_id = gs[:, 8:10, :], gs[:, 10:12, :], gs[:, 2:4, :], gs[:, 4:6, :]
            link(v.tensor_scalar(fits, pos, float(CAP), None, ALU.is_lt))
            link(v.tensor_tensor(gate, gate, fits, ALU.mult))
            link(v.scalar_tensor_tensor(gs[:, 12:14, :], expert_id, float(CAP), pos, ALU.mult, ALU.add))
            link(v.tensor_tensor(cslot[:], gs[:, 12:14, :], fits, ALU.mult))
            link(v.tensor_scalar(gs[:, 12:14, :], pos, float(SP), None, ALU.is_ge))
            link(v.tensor_scalar(gs[:, 14:16, :], pos, float(2 * SP), None, ALU.is_ge))
            link(v.tensor_tensor(gs[:, 12:14, :], gs[:, 12:14, :], gs[:, 14:16, :], ALU.add))
            link(v.scalar_tensor_tensor(etile[:], expert_id, float(SJ), gs[:, 12:14, :], ALU.mult, ALU.add))
            link(v.scalar_tensor_tensor(gs[:, 14:16, :], gs[:, 12:14, :], -float(SP), pos, ALU.mult, ALU.add))
            link(v.scalar_tensor_tensor(gs[:, 12:14, :], gs[:, 14:16, :], 1.0, fits, ALU.add, ALU.mult))
            link(v.tensor_scalar(elane[:], gs[:, 12:14, :], -1.0, None, ALU.add))
            link(v.tensor_scalar(cp1[:], iota_f[0:P, 0:NC], 1.0, None, ALU.add))
            for a in range(2):
                link(v.tensor_tensor(elane_oh[:, a, :, :], iota_f[0:P, 0:SP].unsqueeze(1).broadcast_to([P, NC, SP]),
                                     elane[:, a, :].unsqueeze(2).broadcast_to([P, NC, SP]), ALU.is_equal))
                link(v.tensor_tensor(etile_eq[:, a, :, :], iota_f[0:P, 0:3 * NE].unsqueeze(1).broadcast_to([P, NC, 3 * NE]),
                                     etile[:, a, :].unsqueeze(2).broadcast_to([P, NC, 3 * NE]), ALU.is_equal))
                link(v.tensor_tensor(etile_oh[:, a, :, 0, :], etile_eq[:, a, :, :],
                                     cp1[:].unsqueeze(2).broadcast_to([P, NC, 3 * NE]), ALU.mult))
                link(v.tensor_scalar(etile_oh[:, a, :, 1, :], etile_eq[:, a, :, :], part_f[0:P, 0:1], None, ALU.mult))
            v.engine_nop().then_inc(s_eoh, 1)
            dve.wait_ge(s_einv, 1)
            link(v.tensor_scalar(eidx_f[:, 0, :], ps[0:SP, 6, 0:3 * NE], float(P), -float(P), ALU.mult, ALU.add))
            link(v.tensor_tensor(eidx_f[:, 1, :], eidx_f[:, 0, :], ps[0:SP, 6, 3 * NE:6 * NE], ALU.add))
            v.tensor_scalar(eidx[:, 0:3 * NE], eidx_f[:, 1, :], 0.0, None, ALU.max).then_inc(s_eidx, 1)

            def copy_xd(e, b, n):
                wait_if(dve, s_hid, 2 * e)
                for j in range(SJ):
                    dve.wait_ge(s_xdT, SJ * e + j + 1)
                    v.tensor_copy(xdT[:, :, SP * j:SP * j + SP],
                                  ps[:, j, 0:4 * SP].rearrange("p (a n) -> p a n", a=4)).then_inc(s_xdTsb, 1)

            def expert(e, b, n):
                copy_xd(e + 1, 1 - b, n)
                wait_if(dve, s_yost[b], 16 * n)
                dve.wait_ge(s_eo, 3 * e + 3)
                v.tensor_copy(yo[:, b, 2, :], ps[0:SP, 7, :]).then_inc(s_yov, 1)
            copy_xd(0, 0, 0)
            twos(dve, NE, expert)

            def combine(c, b, n):
                dve.wait_ge(s_ygin[b], 32 * (n + 1))
                wait_if(dve, s_outst[b], 16 * n)
                xc = x[:, bass.ds(c, 1), :].rearrange("p o d -> p (o d)")
                v.scalar_tensor_tensor(ot[:, b, 0, :], yg[:, b, 0, :], gs[:, 2, bass.ds(c, 1)], xc,
                                       ALU.mult, ALU.add).then_inc(s_g1, 1)
                dve.wait_ge(s_g1, c + 1)
                v.scalar_tensor_tensor(ot[:, b, 1, :], yg[:, b, 1, :], gs[:, 3, bass.ds(c, 1)], ot[:, b, 0, :],
                                       ALU.mult, ALU.add).then_inc(s_out, 1)
            twos(dve, NC, combine)

        @block.tensor
        def _(pe):
            mm = nc.tensor.matmul
            pe.wait_ge(s_pool_const, 9)

            pe.wait_ge(s_rowtot, 1)
            mm(ps[0:P, 0, 0:NC], tri[:], cnt[:, 0, :], start=True, stop=True)
            mm(ps[0:P, 0, 16:16 + NC], ones[:], cnt[:, 0, :], start=True, stop=True).then_inc(s_cntmm, 1)

            pe.wait_ge(s_winf, 64)

            def transposes_of_xn(b, bank, signal):
                for m in range(4):
                    part = xn[:, b, 0:C] if m == 0 else xn[:, b, C + m - 1:D:3]
                    ins = nc.tensor.transpose(ps[:, bank, P * m:P * m + P], part, ident[0:P, 0:P])
                ins.then_inc(signal, 1)

            def xn_T(c, b):
                pe.wait_ge(s_xn, c + 1)
                wait_if(pe, s_xT, c - 1)
                transposes_of_xn(b, 6 + b, s_xnT)

            def project(c, b, n, ahead=True):
                if ahead:
                    xn_T(c + 1, 1 - b)
                pe.wait_ge(s_xT, c + 1)
                wait_if(pe, s_tabsb, c - 1)
                for m in range(4):
                    ins = mm(ps[0:P, 4 + b, C * m:C * m + C], xT[:, b, P * m:P * m + P],
                             (win_s_sb if m == 0 else win_v_sb)[:], start=True, stop=True)
                ins.then_inc(s_tabmm, 1)
            xn_T(0, 0)
            project(0, 0, 0)
            project(1, 1, 0)
            with pe.Fori(1, NC // 2 - 1) as i:
                for b in range(2):
                    project(2 * i + b, b, i)
            project(NC - 2, 0, NC // 2 - 1)
            project(NC - 1, 1, NC // 2 - 1, ahead=False)

            def invert(s, b, n, start=False, stop=False):
                pe.wait_ge(s_slotoh, s + 1)
                pe.wait_ge(s_laneoh, s + 1)
                for k in range(KS):
                    ins = mm(ps[:, 1, 0:TILES], lane_oh[:, b, k, :], tile_oh[:, b, k, :],
                             start=start and k == 0, stop=stop and k == KS - 1)
                ins.then_inc(s_invmm, 1)
            invert(0, 0, 0, start=True)
            invert(1, 1, 0)
            with pe.Fori(1, STEPS // 2 - 1) as i:
                for b in range(2):
                    invert(2 * i + b, b, i)
            invert(STEPS - 2, 0, 0)
            invert(STEPS - 1, 1, 0, stop=True)

            def records(q, m4, n4):
                pe.wait_ge(s_recin[m4], 64 * (n4 + 1))
                wait_if(pe, s_fT, q)
                for t in range(HALF):
                    ins = nc.tensor.transpose(ps[0:NRBF, 6, 128 * t:128 * t + 128], rec[:, m4, t, 0:NRBF], ident[:])
                ins.then_inc(s_recT, 1)

            def hidden(q):
                pe.wait_ge(s_fT, q + 1)
                wait_if(pe, s_hread, q)
                mm(ps[:, 7, :], wf1[:], fT[:], start=True, stop=True).then_inc(s_hmm, 1)

            def filters(q, b, t):
                if t == 0:
                    pe.wait_ge(s_h, q + 1)
                wait_if(pe, s_msgv, HALF * q + t - 1)
                mm(ps[:, t % 2, :], h[:, b, 128 * t:128 * t + 128], wf2[:].rearrange("p g c -> p (g c)"),
                   start=True, stop=False)
                mm(ps[:, t % 2, :], ones3[:], bf2_split[:].rearrange("p g c -> p (g c)"),
                   start=False, stop=True).then_inc(s_w, 1)

            def sum_edges(q, m4, t):
                T = HALF * q + t
                pe.wait_ge(s_onehot, T + 1)
                pe.wait_ge(s_msgv, T + 1)
                pe.wait_ge(s_msga, T + 1)
                pair = t // 2
                if t % 2 == 0:
                    wait_if(pe, s_acc, 2 * q + pair - 1)
                for half in range(2):
                    ins = mm(ps[0:P, 2 + 2 * pair + half, :], onehot[:, HALF * (m4 % 2) + t, :],
                             msg[:, t, 4 * half:4 * half + 4, :].rearrange("p m c -> p (m c)"),
                             start=t % 2 == 0, stop=t % 2 == 1)
                ins.then_inc(s_scat, 1)

            pe.wait_ge(s_tabsb, NC)
            pe.wait_ge(s_wprep, 1)
            records(0, 0, 0)
            hidden(0)
            records(1, 1, 0)
            filters(0, 0, 0)
            filters(0, 0, 1)

            def step(q, m4, n4, n2):
                b = m4 % 2
                hidden(q + 1)
                filters(q, b, 2)
                sum_edges(q, m4, 0)
                filters(q, b, 3)
                sum_edges(q, m4, 1)
                filters(q + 1, 1 - b, 0)
                sum_edges(q, m4, 2)
                records(q + 2, (m4 + 2) % 4, n4 + (m4 + 2) // 4)
                filters(q + 1, 1 - b, 1)
                sum_edges(q, m4, 3)
            halves(pe, step)

            pe.wait_ge(s_acc, PAIRS)

            def sums_T(c, b, n):
                pe.wait_ge(s_aggc, c + 1)
                wait_if(pe, s_aTv, c - 1)
                wait_if(pe, s_aTa, c - 1)
                for m in range(8):
                    ins = nc.tensor.transpose(ps[:, 2 * b + m // 4, P * (m % 4):P * (m % 4) + P],
                                              aggc[:, b, m, :], ident[0:P, 0:P])
                ins.then_inc(s_aggT, 1)

            def products(c, b, n):
                pe.wait_ge(s_aTv, c + 1)
                pe.wait_ge(s_aTa, c + 1)
                wait_if(pe, s_x1, c - 1)
                wait_if(pe, s_vT, c - 1)
                mm(ps[:, 6 + b, 0:P], w1[:, 0, 0, :], aT[:, b, 0, :], start=True, stop=False)
                mm(ps[:, 6 + b, 0:P], w1[:, 0, 1, :], aT[:, b, 4, :], start=False, stop=True)
                mm(ps[:, 4 + b, P:4 * P], w1[:, 1, 0, :], aT[:, b, 5:8, :].rearrange("p m n -> p (m n)"),
                   start=True, stop=False)
                mm(ps[:, 4 + b, P:4 * P], w1[:, 1, 1, :], aT[:, b, 1:4, :].rearrange("p m n -> p (m n)"),
                   start=False, stop=True).then_inc(s_sv, 1)

            def outputs(c, b, n):
                pe.wait_ge(s_spT, c + 1)
                pe.wait_ge(s_vT, c + 1)
                mm(ps[0:P, 6 + b, 0:C], spT[:, b, :], w2[:, 0, :], start=True, stop=True)
                for i in range(3):
                    ins = mm(ps[0:P, 6 + b, C * (i + 1):C * (i + 2)], vT[:, b, i, :], w2[:, 1, :], start=True, stop=True)
                ins.then_inc(s_o, 1)

            def chunk(c, b, n):
                sums_T(c, b, n)
                products(c, b, n)
                outputs(c, b, n)
            twos(pe, NC, chunk)

            def logits(c, b, n):
                pe.wait_ge(s_yn, c + 1)
                wait_if(pe, s_yT, c - 1)
                for m in range(4):
                    ins = nc.tensor.transpose(ps[:, b, P * m:P * m + P], xn[:, b, C * m:C * m + C], ident[0:P, 0:P])
                ins.then_inc(s_ynT, 1)
                pe.wait_ge(s_yT, c + 1)
                wait_if(pe, s_lg, c - 1)
                for m in range(4):
                    ins = mm(ps[0:P, 2 + b, 0:NE], xT[:, b, P * m:P * m + P], wg[:, m, :], start=m == 0, stop=m == 3)
                ins.then_inc(s_lgmm, 1)
            twos(pe, NC, logits)

            pe.wait_ge(s_masks, 1)
            masks = g[:, 4:6, :, :].rearrange("p a c e -> p (a c e)")
            mm(ps[0:P, 4, 0:320], tri[:], masks, start=True, stop=True)
            mm(ps[0:P, 5, 0:320], ones[:], masks, start=True, stop=True).then_inc(s_cum, 1)
            pe.wait_ge(s_eoh, 1)
            for a in range(2):
                for c in range(NC):
                    ins = mm(ps[0:SP, 6, 0:6 * NE], elane_oh[:, a, c, :],
                             etile_oh[:, a, c, :, :].rearrange("p w t -> p (w t)"),
                             start=a == 0 and c == 0, stop=a == 1 and c == NC - 1)
            ins.then_inc(s_einv, 1)

            def tokens_T(e, b, n):
                pe.wait_ge(s_xdin[b], 48 * (n + 1))
                for j in range(SJ):
                    wait_if(pe, s_xdTsb, SJ * (e - 1) + j + 1)
                    for m in range(4):
                        ins = nc.tensor.transpose(ps[:, j, SP * m:SP * m + SP], xd[:, b, j, C * m:C * m + C],
                                                  ident[0:SP, 0:SP])
                    ins.then_inc(s_xdT, 1)
            pe.wait_ge(s_eidx, 1)
            tokens_T(0, 0, 0)

            def expert(e, b, n):
                pe.wait_ge(s_we[b], 32 * (n + 1))
                pe.wait_ge(s_xdTsb, SJ * e + SJ)
                for a in range(2):
                    wait_if(pe, s_hT, 2 * (e - 1) + a + 1)
                    for m in range(4):
                        ins = mm(ps[:, 3 + a, 0:CAP], we1[:, b, m, 128 * a:128 * a + 128], xdT[:, m, :],
                                 start=m == 0, stop=m == 3)
                    ins.then_inc(s_hid, 1)
                tokens_T(e + 1, 1 - b, n + b)
                pe.wait_ge(s_hT, 2 * e + 2)
                for j in range(SJ):
                    if j < 2:
                        wait_if(pe, s_yoa, 2 * (e - 1) + j + 1)
                    else:
                        wait_if(pe, s_yov, e)
                    for a in range(2):
                        ins = mm(ps[0:SP, 5 + j, :], hT[:, a, SP * j:SP * j + SP], we2[:, b, a, :],
                                 start=a == 0, stop=a == 1)
                    ins.then_inc(s_eo, 1)
            twos(pe, NE, expert)


_INS = ["x", "src", "dst", "edge_attr_20", "edge_attr_3", "edge_weight", "L0_gnn_W_in2f_s", "L0_gnn_W_in2f_v",
        "L0_gnn_Wf1", "L0_gnn_bf1", "L0_gnn_Wf2", "L0_gnn_bf2", "L0_gnn_W1_s", "L0_gnn_W1_v", "L0_gnn_W2_s",
        "L0_gnn_W2_v", "L0_ffn_w_gating", "L0_ffn_w1", "L0_ffn_w2"]


def kernel(**inputs):
    import numpy as _np
    import concourse.bacc as _bacc
    from concourse import mybir as _mybir
    from concourse.bass_utils import run_bass_kernel_spmd as _run

    nc = _bacc.Bacc("TRN2", target_bir_lowering=False, num_devices=1)
    arrays, args = {}, []
    for name in _INS:
        a = _np.ascontiguousarray(inputs[name])
        arrays[f"in_{name}_dram"] = a
        args.append(nc.dram_tensor(f"in_{name}_dram", a.shape, _mybir.dt.from_np(a.dtype), kind="ExternalInput").ap())
    out = nc.dram_tensor("out_dram", (N, D), F32, kind="ExternalOutput").ap()
    build(nc, *args, out)
    r = _run(nc, [arrays], core_ids=[0])
    return r.results[0]["out_dram"]
```

```python
import concourse.bass as bass
from concourse import mybir
from contextlib import ExitStack
import numpy as np

F32 = mybir.dt.float32
BF16 = mybir.dt.bfloat16
I32 = mybir.dt.int32
U32 = mybir.dt.uint32
ALU = mybir.AluOpType
ACT = mybir.ActivationFunctionType
AX = mybir.AxisListType

N = 1250
E = 21250
D = 512
C = 128
NRBF = 20
P = 125
NC = N // P
EC = E // P
HALF = 4
PAIRS = (E + NC * 255) // 256
TILES = 2 * PAIRS
HALVES = TILES // HALF
PEEL = 6
LOOPS = (HALVES - PEEL) // 4
SLOTCOLS = (HALVES + 2) * HALF
REC, USED = 128 // HALF, 26
R_W, R_U, R_DST, R_SRC = 20, 21, 24, 25
KS = 5
KS_ACT = 4
STEPS = EC // KS
NE = 16
CAP = min(N, N * 4 // NE)
SJ = 3
SP = CAP // SJ
RING = 4
HID = 256
LN2 = float(np.log(2.0))
EPS = 1e-5
Y0 = float(1.0 / np.sqrt(4.0 * np.pi))
Y1 = float(np.sqrt(3.0 / (4.0 * np.pi)))

assert TILES % HALF == 0 and (HALVES - PEEL) % 4 == 0 and STEPS % 2 == 0 and CAP % SJ == 0 and TILES < 256 and EC < 256


def wait_if(eng, sem, value):
    if isinstance(value, int) and value <= 0:
        return
    eng.wait_ge(sem, value)


def wait_apart(eng, sem, value, tick):
    if isinstance(value, int):
        wait_if(eng, sem, value)
    else:
        eng.wait_ge(sem, value)
        eng.sem_inc(tick)


def build(nc, x_in, src_in, dst_in, ea_in, ev_in, ew_in, win_s, win_v, wf1_in, bf1_in, wf2_in, bf2_in,
          w1s_in, w1v_in, w2s_in, w2v_in, wg_in, we1_in, we2_in, out):
    ctx = ExitStack()
    with ctx:
        def sb(name, shape, dt=F32):
            return ctx.enter_context(nc.sbuf_tensor(name, shape, dt))

        def sem(name):
            return ctx.enter_context(nc.semaphore(name))

        def carve(flat):
            used = [0]

            def piece(parts, shape, dt=F32):
                n = int(np.prod(shape))
                words = n if dt != BF16 else n // 2
                ap = flat[0:parts, used[0]:used[0] + words]
                used[0] += words
                assert used[0] <= flat.shape[1] and words * (1 if dt != BF16 else 2) == n
                if dt != F32:
                    ap = ap.bitcast(dt)
                names = "abcdef"[:len(shape)]
                if len(shape) > 1:
                    ap = ap.rearrange(f"p ({' '.join(names)}) -> p {' '.join(names)}",
                                      **dict(zip(names, shape)))
                return ap
            return piece

        node_tab = nc.dram_tensor("node_tab", [N, D], F32).ap()
        edge_tab = nc.dram_tensor("edge_tab", [E, REC], F32).ap()
        y_tab = nc.dram_tensor("y_tab", [N, D], F32).ap()
        expert_tab = nc.dram_tensor("expert_tab", [NE * CAP, D], F32).ap()

        iota_i = sb("iota_i", [128, 256], I32)
        iota_f = sb("iota_f", [128, 256])
        edge_i = sb("edge_i", [P, EC], I32)
        edge_w = sb("edge_w", [P, EC])
        part_i = sb("part_i", [128, 1], I32)
        part_f = sb("part_f", [128, 1])
        ident = sb("ident", [128, 128])
        tri = sb("tri", [P, P])
        ones = sb("ones", [P, P])
        ones3 = sb("ones3", [3, 128], BF16)
        win_s_sb = sb("win_s_sb", [C, C])
        win_v_sb = sb("win_v_sb", [C, C])
        wf1 = sb("wf1", [128, HALF, C])
        bf1 = sb("bf1", [C, 1])
        wf2_raw = sb("wf2_raw", [C, 4 * C])
        wf2 = sb("wf2", [C, 4, C])
        bf2_raw = sb("bf2_raw", [3, 4 * C])
        bf2_rest = sb("bf2_rest", [3, 4 * C])
        bf2_parts = sb("bf2_parts", [3, 3, 4 * C], BF16)
        bf2_split = sb("bf2_split", [3, 4, C], BF16)
        w1_raw = sb("w1_raw", [C, 2, 2, C])
        w1 = sb("w1", [C, 2, 2, C])
        w2_raw = sb("w2_raw", [C, 2, C])
        w2 = sb("w2", [C, 2, C])
        wg = sb("wg", [C, 4, NE])
        we1 = sb("we1", [128, 2, 4, HID])
        we2 = sb("we2", [128, 2, 2, D])
        x = sb("x", [P, NC, D])
        stats = sb("stats", [P, NC, 6])
        ln_t = sb("ln_t", [P, 6, NC])
        rstd = sb("rstd", [P, NC])
        shift = sb("shift", [P, NC])
        xn = sb("xn", [P, 2, D])
        xT = sb("xT", [128, 2, 4 * P])
        tab_sb = sb("tab_sb", [P, 2, D])
        region = sb("region", [128, NC * 8 * C])
        agg = region[0:P, :].rearrange("p (c m) -> p c m", c=NC)
        o = 0
        ea = region[0:P, o:o + EC * NRBF].rearrange("p (k f) -> p k f", f=NRBF)
        o += EC * NRBF
        ge = region[0:P, o:o + (NC + 1) * EC].rearrange("p (b k) -> p b k", b=NC + 1)
        o += (NC + 1) * EC
        ind_flat = region[0:P, o:o + NC * EC]
        ind = ind_flat.rearrange("p (b k) -> p b k", b=NC)
        o += NC * EC
        incl_flat = region[0:P, o:o + NC * EC]
        incl = incl_flat.rearrange("p (b k) -> p b k", b=NC)
        assert o + NC * EC <= NC * 8 * C
        bin_reset = sb("bin_reset", [P, NC, EC])
        ev = sb("ev", [P, EC, 3])
        ew = sb("ew", [P, EC])
        src_i = sb("src_i", [P, EC], I32)
        dst_i = sb("dst_i", [P, EC], I32)
        srcf = sb("srcf", [P, EC])
        chunkf = sb("chunkf", [P, EC])
        lane_f = sb("lane_f", [P, EC])
        lane_neg = sb("lane_neg", [P, EC])
        tile_f = sb("tile_f", [P, EC])
        cnt = sb("cnt", [P, 8, NC])
        cnt_i = sb("cnt_i", [P, NC], I32)
        thr = sb("thr", [P, NC + 1])
        shared = sb("shared", [128, EC * (REC + 4 + 3) + KS * (128 + 2 * TILES) + 2 * KS_ACT * 128])
        early = carve(shared)
        rec_all = early(P, [EC, REC])
        nrm = early(P, [4, EC])
        slot_i = early(P, [3, EC], I32)
        lane_oh = early(P, [2, KS, 128], BF16)
        lane_abs = early(P, [2, KS_ACT, 128])
        tile_oh = early(P, [2, KS, TILES])
        idx_all = sb("idx_all", [128, SLOTCOLS], U32)
        idx_f = sb("idx_f", [128, TILES])
        valid = sb("valid", [128, SLOTCOLS])
        pair_ge = sb("pair_ge", [1, PAIRS, NC])
        pair_f = sb("pair_f", [1, 2, PAIRS])
        pair_chunk = sb("pair_chunk", [1, PAIRS], I32)
        idx4 = sb("idx4", [128, 2, HALF], U32)
        rec = sb("rec", [128, 4, HALF, REC])
        rec_u = rec[:].bitcast(U32)
        rv = sb("rv", [128, 2, HALF])
        onehot = sb("onehot", [128, 8, P])
        loop = carve(shared)
        xg = loop(128, [8, 4, C])
        fT = sb("fT", [128, 128])
        sp_t = sb("sp_t", [128, 3, 512])
        h = sb("h", [128, 2, 512])
        dot = sb("dot", [128, 3, C])
        msg = loop(128, [4, 9, C])
        chunks = carve(shared)
        aggc = chunks(P, [2, 8 * C])
        aT = chunks(C, [2, 8, P])
        sT = sb("sT", [C, 3, P])
        spT = sb("spT", [C, 2, P])
        vT = sb("vT", [C, 2, 3, P])
        late = carve(region)
        g = late(P, [10, NC, NE])
        gs = late(P, [16, NC])
        reset = late(P, [NE, NC])
        totT = late(P, [2, NE, NC])
        preT = late(P, [2, NE, NC])
        elane_oh = late(P, [2, NC, SP], BF16)
        etile_eq = late(P, [2, NC, 3 * NE], BF16)
        etile_oh = late(P, [2, NC, 2, 3 * NE], BF16)
        xdT = late(128, [4, CAP])
        hT = late(128, [2, CAP])
        elane = sb("elane", [P, 2, NC])
        etile = sb("etile", [P, 2, NC])
        cp1 = sb("cp1", [P, NC])
        eidx_f = sb("eidx_f", [SP, 2, 3 * NE])
        eidx = sb("eidx", [SP, 3 * (NE + 1)], U32)
        eidx3 = sb("eidx3", [SP, 2, 3], U32)
        cslot = sb("cslot", [P, 2, NC], U32)
        rows = carve(shared)
        xd = rows(SP, [2, SJ, D])
        yo = rows(SP, [2, SJ, D])
        yg = carve(shared)(P, [RING, 2, D])

        ps = ctx.enter_context(nc.psum_tensor("ps", [128, 8, 512], F32))

        s_sp_tick = sem("s_sp_tick")
        s_pool_tick = sem("s_pool_tick")
        s_pool_step = sem("s_pool_step")
        s_xin = sem("s_xin")
        s_srcin = sem("s_srcin")
        s_evin = sem("s_evin")
        s_eain = sem("s_eain")
        s_win = sem("s_win")
        s_winf = sem("s_winf")
        s_pool_const = sem("s_pool_const")
        s_dve = sem("s_dve")
        s_stats = sem("s_stats")
        s_sqrt = sem("s_sqrt")
        s_norm = sem("s_norm")
        s_nrm2 = sem("s_nrm2")
        s_xn = sem("s_xn")
        s_xnT = sem("s_xnT")
        s_xT = sem("s_xT")
        s_tabmm = sem("s_tabmm")
        s_tabsb = sem("s_tabsb")
        s_tabst = [sem(f"s_tabst{b}") for b in range(2)]
        s_wprep = sem("s_wprep")
        s_recf = sem("s_recf")
        s_recv = sem("s_recv")
        s_rect = sem("s_rect")
        s_reset = sem("s_reset")
        s_zeros = sem("s_zeros")
        s_wf1in = sem("s_wf1in")
        s_unit = sem("s_unit")
        s_rowtot = sem("s_rowtot")
        s_cntmm = sem("s_cntmm")
        s_slotoh = sem("s_slotoh")
        s_lane = sem("s_lane")
        s_labs = sem("s_labs")
        s_laneoh = sem("s_laneoh")
        s_invmm = sem("s_invmm")
        s_idx = sem("s_idx")
        s_agg0 = sem("s_agg0")
        s_idx4 = sem("s_idx4")
        s_recin = [sem(f"s_recin{b}") for b in range(4)]
        s_xgin = [sem(f"s_xgin{b}") for b in range(2)]
        s_rv = sem("s_rv")
        s_onehot = sem("s_onehot")
        s_recT = sem("s_recT")
        s_fT = sem("s_fT")
        s_hmm = sem("s_hmm")
        s_hread = sem("s_hread")
        s_act = sem("s_act")
        s_sp = sem("s_sp")
        s_h = sem("s_h")
        s_w = sem("s_w")
        s_sc = sem("s_sc")
        s_dot = sem("s_dot")
        s_dot3 = sem("s_dot3")
        s_msgv = sem("s_msgv")
        s_msga = sem("s_msga")
        s_scat = sem("s_scat")
        s_acc = sem("s_acc")
        s_aggc = sem("s_aggc")
        s_aggT = sem("s_aggT")
        s_aTv = sem("s_aTv")
        s_aTa = sem("s_aTa")
        s_sv = sem("s_sv")
        s_spa = sem("s_spa")
        s_spT = sem("s_spT")
        s_vT = sem("s_vT")
        s_o = sem("s_o")
        s_x1 = sem("s_x1")
        s_yn = sem("s_yn")
        s_ynT = sem("s_ynT")
        s_yT = sem("s_yT")
        s_yst = [sem(f"s_yst{b}") for b in range(2)]
        s_lgmm = sem("s_lgmm")
        s_lg = sem("s_lg")
        s_gmax = sem("s_gmax")
        s_gexp = sem("s_gexp")
        s_masks = sem("s_masks")
        s_cum = sem("s_cum")
        s_eoh = sem("s_eoh")
        s_einv = sem("s_einv")
        s_eidx = sem("s_eidx")
        s_we = [sem(f"s_we{b}") for b in range(2)]
        s_e3 = sem("s_e3")
        s_xdin = [sem(f"s_xdin{b}") for b in range(2)]
        s_xdT = sem("s_xdT")
        s_xdTsb = sem("s_xdTsb")
        s_hid = sem("s_hid")
        s_hT = sem("s_hT")
        s_eo = sem("s_eo")
        s_yoa = sem("s_yoa")
        s_yov = sem("s_yov")
        s_yost = [sem(f"s_yost{b}") for b in range(2)]
        s_ygin = [sem(f"s_ygin{b}") for b in range(RING)]
        s_out = sem("s_out")
        s_outst = sem("s_outst")

        block = ctx.enter_context(nc.Block())

        def halves(eng, step, last=None):
            for q in range(PEEL):
                step(q, q % 4, q // 4, q // 2)
            with eng.Fori(0, LOOPS) as i:
                for k in range(PEEL, PEEL + 4):
                    step(4 * i + k, k % 4, i + k // 4, 2 * i + k // 2)

        def twos(eng, count, step):
            for c in range(2):
                step(c, c, 0)
            with eng.Fori(1, count // 2) as i:
                for b in range(2):
                    step(2 * i + b, b, i)

        def ahead(eng, count, step):
            for c in range(2):
                step(c, c, 0, lambda k: True)
            with eng.Fori(1, count // 2 - 1) as i:
                for b in range(2):
                    step(2 * i + b, b, i, lambda k: True)
            for c in range(count - 2, count):
                step(c, c % 2, c // 2, lambda k, c=c: c + k < count)

        @block.sync
        def _(sp):
            sp.dma_start(src_i[:], src_in.rearrange("(p k) -> p k", k=EC)).then_inc(s_srcin, 16)
            sp.dma_start(x[:], x_in.rearrange("(c p) d -> p c d", p=P)).then_inc(s_xin, 16)
            sp.dma_start(ev[:], ev_in.rearrange("(p k) i -> p k i", k=EC)).then_inc(s_evin, 16)
            sp.dma_start(ew[:], ew_in.rearrange("(p k) -> p k", k=EC)).then_inc(s_evin, 16)
            sp.dma_start(dst_i[:], dst_in.rearrange("(p k) -> p k", k=EC)).then_inc(s_evin, 16)
            sp.dma_start(wf2_raw[:], wf2_in[:, 0:4 * C]).then_inc(s_win, 16)
            for r in range(3):
                sp.dma_start(bf2_raw[r:r + 1, :], bf2_in[0:4 * C].rearrange("(a n) -> a n", a=1)).then_inc(s_win, 16)
            sp.dma_start(w1_raw[:, 0, :, :], w1s_in.rearrange("(f t) c -> f t c", t=2)).then_inc(s_win, 16)
            sp.dma_start(w1_raw[:, 1, :, :], w1v_in.rearrange("(f t) c -> f t c", t=2)).then_inc(s_win, 16)
            sp.dma_start(w2_raw[:, 0, :], w2s_in).then_inc(s_win, 16)
            sp.dma_start(w2_raw[:, 1, :], w2v_in).then_inc(s_win, 16)
            sp.dma_start(wg[:], wg_in.rearrange("(a f) e -> f a e", f=C)).then_inc(s_win, 16)

            def store_tab(c, b, n):
                wait_apart(sp, s_tabsb, c + 1, s_sp_tick)
                sp.dma_start(node_tab[bass.ds(P * c, P), :], tab_sb[:, b, :]).then_inc(s_tabst[b], 16)
            twos(sp, NC, store_tab)
            sp.wait_ge(s_recf, 1)
            sp.wait_ge(s_recv, 1)
            sp.dma_start(edge_tab.rearrange("(p k) r -> p k r", k=EC), rec_all[:]).then_inc(s_rect, 16)

            def load_expert(e, b):
                sp.dma_start(we1[:, b, :, :].rearrange("p a h -> p (a h)").rearrange("p (a h) -> p a h", a=4),
                             we1_in[bass.ds(e, 1), :, :].rearrange("o (a p) h -> p (o a) h", p=128)).then_inc(s_we[b], 16)
                sp.dma_start(we2[:, b, :, :],
                             we2_in[bass.ds(e, 1), :, :].rearrange("o (a p) d -> p (o a) d", p=128)).then_inc(s_we[b], 16)
            load_expert(0, 0)
            load_expert(1, 1)

            def store_y(c, b, n):
                wait_apart(sp, s_yn, c + 1, s_sp_tick)
                sp.dma_start(y_tab[bass.ds(P * c, P), :], xn[:, b, :]).then_inc(s_yst[b], 16)
            twos(sp, NC, store_y)

            def expert(e, b, n):
                wait_apart(sp, s_yoa, 2 * e + 2, s_sp_tick)
                wait_apart(sp, s_yov, e + 1, s_sp_tick)
                sp.dma_start(expert_tab[bass.ds(CAP * e, CAP), :].rearrange("(j p) d -> p j d", p=SP),
                             yo[:, b, :, :]).then_inc(s_yost[b], 16)

            def expert_and_load(e, b, n):
                expert(e, b, n)
                load_expert(e + 2, b)
            for e in range(2):
                expert_and_load(e, e, 0)
            with sp.Fori(1, NE // 2 - 1) as i:
                for b in range(2):
                    expert_and_load(2 * i + b, b, i)
            for e in range(NE - 2, NE):
                expert(e, e % 2, e // 2)

            for c in range(NC):
                sp.wait_ge(s_out, c + 1)
                sp.dma_start(out[P * c:P * c + P, :], x[:, c, :]).then_inc(s_outst, 16)
            sp.wait_ge(s_outst, 16 * NC)

        @block.gpsimd
        def _(pool):
            nc.gpsimd.iota(iota_i[:], pattern=[[1, 256]], base=0, channel_multiplier=0).then_inc(s_pool_const, 1)
            nc.gpsimd.iota(edge_i[:], pattern=[[1, EC]], base=0, channel_multiplier=EC).then_inc(s_pool_const, 1)
            nc.gpsimd.iota(part_i[:], pattern=[[1, 1]], base=0, channel_multiplier=1).then_inc(s_pool_const, 1)
            nc.gpsimd.memset(ident[:], 0.0).then_inc(s_pool_const, 1)
            nc.gpsimd.memset(tri[:], 1.0).then_inc(s_pool_const, 1)
            nc.gpsimd.memset(ones[:], 1.0).then_inc(s_pool_const, 1)
            nc.gpsimd.memset(ones3[:], 1.0).then_inc(s_pool_const, 1)
            nc.gpsimd.memset(wf1[:], 0.0).then_inc(s_zeros, 1)
            nc.gpsimd.memset(rec_all[:, :, USED:REC], 0.0)
            nc.gpsimd.memset(bin_reset[:], 1.0).then_inc(s_reset, 1)
            pool.wait_ge(s_reset, 1)
            nc.gpsimd.memset(bin_reset[:, :, 0:1], 0.0).then_inc(s_reset, 1)
            pool.wait_ge(s_pool_const, 7)
            nc.gpsimd.affine_select(out=ident[:], in_=ident[:], compare_op=ALU.not_equal, fill=1.0, base=0,
                                    pattern=[[-1, 128]], channel_multiplier=1).then_inc(s_pool_const, 1)
            nc.gpsimd.affine_select(out=tri[:], in_=tri[:], compare_op=ALU.is_gt, fill=0.0, base=0,
                                    pattern=[[1, P]], channel_multiplier=-1).then_inc(s_pool_const, 1)

            pc = [0]

            def link(ins):
                pc[0] += 1
                ins.then_inc(s_pool_step, 1)
                pool.wait_ge(s_pool_step, pc[0])

            g_ = nc.gpsimd
            pool.wait_ge(s_win, 16 * 9)
            for part, (first, odd) in enumerate(((0, 0), (2 * C, 0), (0, 1), (2 * C, 1))):
                g_.tensor_copy(wf2[:, part, :], wf2_raw[:, first + odd:first + 2 * C:2])
            link(g_.tensor_copy(bf2_parts[:, 0, :], bf2_raw[:]))
            link(g_.tensor_tensor(bf2_rest[:], bf2_raw[:], bf2_parts[:, 0, :], ALU.subtract))
            link(g_.tensor_copy(bf2_parts[:, 1, :], bf2_rest[:]))
            link(g_.tensor_tensor(bf2_rest[:], bf2_rest[:], bf2_parts[:, 1, :], ALU.subtract))
            link(g_.tensor_copy(bf2_parts[:, 2, :], bf2_rest[:]))
            for j in range(3):
                link(g_.tensor_scalar(bf2_parts[:, j, :], bf2_parts[:, j, :], ident[0:3, j:j + 1], None, ALU.mult))
            for j in (1, 2):
                link(g_.tensor_tensor(bf2_parts[:, 0, :], bf2_parts[:, 0, :], bf2_parts[:, j, :], ALU.add))
            for part, (first, odd) in enumerate(((0, 0), (2 * C, 0), (0, 1), (2 * C, 1))):
                g_.tensor_copy(bf2_split[:, part, :], bf2_parts[:, 0, first + odd:first + 2 * C:2])
            both = 1.0 / np.sqrt(2.0 * C) / np.sqrt(float(C))
            for kind, odd, scale in ((0, 0, Y0), (0, 1, Y1 / np.sqrt(3.0)), (1, 0, Y1), (1, 1, Y0)):
                g_.tensor_scalar(w1[:, kind, odd, :], w1_raw[:, kind, odd, :], float(scale * both), None, ALU.mult)
            link(g_.tensor_scalar(w2[:], w2_raw[:], float(1.0 / np.sqrt(float(C))), None, ALU.mult))
            pool.wait_ge(s_evin, 48)
            g_.tensor_copy(rec_all[:, :, R_W], ew[:])
            g_.tensor_copy(rec_all[:, :, R_DST].bitcast(I32), dst_i[:])
            pool.wait_ge(s_unit, 1)
            g_.tensor_tensor(rec_all[:, :, R_U:R_U + 3], ev[:], nrm[:, 1, :].unsqueeze(2).broadcast_to([P, EC, 3]),
                             ALU.mult).then_inc(s_recv, 1)
            pool.wait_ge(s_recf, 1)
            pool.wait_ge(s_recv, 1)
            g_.memset(agg, 0.0).then_inc(s_wprep, 1)

            def gather_rec(q, m4, n4, n2):
                b = m4 % 2
                nc.gpsimd.tensor_copy(idx4[:, b, :], idx_all[:, bass.ds(HALF * q, HALF)]).then_inc(s_idx4, 1)
                wait_apart(pool, s_idx4, q + 1, s_pool_tick)
                wait_apart(pool, s_scat, HALF * (q - 3), s_pool_tick)
                for t in range(HALF):
                    nc.gpsimd.indirect_dma_start(
                        rec[:, m4, t, :], None, edge_tab,
                        bass.IndirectOffsetOnAxis(ap=idx4[:, b, t:t + 1], axis=0)).then_inc(s_recin[m4], 16)

            def gather_xg(q, m4, n4, n2):
                wait_apart(pool, s_recin[m4], 64 * (n4 + 1), s_pool_tick)
                for t in range(HALF):
                    slot = HALF * (m4 % 2) + t
                    wait_apart(pool, s_msgv, HALF * (q - 2) + t + 1, s_pool_tick)
                    nc.gpsimd.indirect_dma_start(
                        xg[:, slot, :, :].rearrange("p a c -> p (a c)"), None, node_tab,
                        bass.IndirectOffsetOnAxis(ap=rec_u[:, m4, t, R_DST:R_DST + 1], axis=0)
                    ).then_inc(s_xgin[m4 % 2], 16)

            def weights_of(q, m4, n4, n2):
                wait_apart(pool, s_onehot, HALF * (q - 1), s_pool_tick)
                nc.gpsimd.tensor_tensor(rv[:, m4 % 2, :], rec[:, m4, :, R_W],
                                        valid[:, bass.ds(HALF * q, HALF)], ALU.mult).then_inc(s_rv, 1)

            pool.wait_ge(s_idx, 1)
            pool.wait_ge(s_rect, 16)
            gather_rec(0, 0, 0, 0)
            gather_rec(1, 1, 0, 0)
            for b in range(2):
                pool.wait_ge(s_tabst[b], 16 * (NC // 2))
            gather_xg(0, 0, 0, 0)
            weights_of(0, 0, 0, 0)

            def step(q, m4, n4, n2):
                gather_rec(q + 2, (m4 + 2) % 4, n4 + (m4 + 2) // 4, n2 + 1)
                gather_xg(q + 1, (m4 + 1) % 4, n4 + (m4 + 1) // 4, n2 + (m4 + 1) // 2 - m4 // 2)
                weights_of(q + 1, (m4 + 1) % 4, n4 + (m4 + 1) // 4, n2)
            halves(pool, step)
            pool.wait_ge(s_recin[(HALVES + 1) % 4], 64 * ((HALVES + 1) // 4 + 1))
            pool.wait_ge(s_xgin[HALVES % 2], 64 * (HALVES // 2 + 1))

            pool.wait_ge(s_acc, PAIRS)

            def copy_agg(j, b, n):
                if not isinstance(j, int) or j >= 2:
                    wait_apart(pool, s_aggT, j + 1, s_pool_tick)
                nc.gpsimd.tensor_copy(aggc[:, b, :], agg[:, bass.ds(j + 2, 1), :].rearrange("p o m -> p (o m)")).then_inc(s_aggc, 1)
            twos(pool, NC - 2, copy_agg)

            pool.wait_ge(s_eidx, 1)
            for b in range(2):
                pool.wait_ge(s_yst[b], 16 * (NC // 2))

            def gather_tokens(e, b, n):
                wait_apart(pool, s_xdT, 3 * (e - 1), s_pool_tick)
                nc.gpsimd.tensor_copy(eidx3[:, b, :], eidx[:, bass.ds(SJ * e, SJ)]).then_inc(s_e3, 1)
                wait_apart(pool, s_e3, e + 1, s_pool_tick)
                for j in range(SJ):
                    nc.gpsimd.indirect_dma_start(
                        xd[:, b, j, :], None, y_tab,
                        bass.IndirectOffsetOnAxis(ap=eidx3[:, b, j:j + 1], axis=0)).then_inc(s_xdin[b], 16)
            twos(pool, NE, gather_tokens)
            gather_tokens(NE, NE % 2, NE // 2)

            for b in range(2):
                pool.wait_ge(s_yost[b], 16 * (NE // 2))
            pool.wait_ge(s_xdin[NE % 2], 48 * (NE // 2 + 1))

            pool.wait_ge(s_xdT, SJ * (NE + 1))
            for c in range(NC):
                wait_if(pool, s_out, c - RING + 1)
                for a in range(2):
                    nc.gpsimd.indirect_dma_start(
                        yg[:, c % RING, a, :], None, expert_tab,
                        bass.IndirectOffsetOnAxis(ap=cslot[:, a, c:c + 1], axis=0)).then_inc(s_ygin[c % RING], 16)

        @block.scalar
        def _(act):
            chain = [0]

            def link(ins):
                chain[0] += 1
                ins.then_inc(s_act, 1)
                act.wait_ge(s_act, chain[0])

            act.dma_start(ea, ea_in.rearrange("(p k) f -> p k f", k=EC)).then_inc(s_eain, 16)
            act.dma_start(win_s_sb[:], win_s).then_inc(s_winf, 16)
            act.dma_start(win_v_sb[:], win_v).then_inc(s_winf, 16)
            act.dma_start(bf1[:], bf1_in.rearrange("(c a) -> c a", a=1)).then_inc(s_winf, 16)
            act.wait_ge(s_zeros, 1)
            for t in range(HALF):
                act.dma_start(wf1[REC * t:REC * t + NRBF, t, :], wf1_in).then_inc(s_wf1in, 16)

            act.wait_ge(s_eain, 16)
            nc.scalar.copy(rec_all[:, :, 0:NRBF], ea).then_inc(s_recf, 1)

            act.wait_ge(s_stats, 1)
            nc.scalar.activation(ln_t[:, 3, :], ln_t[:, 2, :], ACT.Sqrt).then_inc(s_sqrt, 1)
            act.wait_ge(s_nrm2, 1)
            nc.scalar.activation(nrm[:, 1, :], nrm[:, 0, :], ACT.Sqrt).then_inc(s_sqrt, 1)

            act.wait_ge(s_norm, 1)

            def norm_x(c, b):
                wait_if(act, s_xnT, c - 1)
                nc.scalar.activation(xn[:, b, :], x[:, bass.ds(c, 1), :].rearrange("p o d -> p (o d)"), ACT.Identity,
                                     bias=shift[:, bass.ds(c, 1)], scale=rstd[:, bass.ds(c, 1)]).then_inc(s_xn, 1)

            def copy_xT(c, b):
                act.wait_ge(s_xnT, c + 1)
                wait_if(act, s_tabmm, c - 1)
                nc.scalar.copy(xT[:, b, :], ps[:, 6 + b, 0:4 * P]).then_inc(s_xT, 1)

            def copy_tab(c, b, n):
                act.wait_ge(s_tabmm, c + 1)
                wait_if(act, s_tabst[b], 16 * n)
                nc.scalar.copy(tab_sb[:, b, :], ps[0:P, 4 + b, :]).then_inc(s_tabsb, 1)

            norm_x(0, 0)
            norm_x(1, 1)
            copy_xT(0, 0)

            def project(c, b, n, more):
                if more(1):
                    copy_xT(c + 1, 1 - b)
                if more(2):
                    norm_x(c + 2, b)
                copy_tab(c, b, n)
            ahead(act, NC, project)

            act.wait_ge(s_lane, 1)

            def lane_distance(j, b):
                wait_if(act, s_laneoh, j - 1)
                for k in range(KS_ACT):
                    ins = nc.scalar.activation(lane_abs[:, b, k, :], iota_f[0:P, 0:128], ACT.Abs,
                                               bias=lane_neg[:, bass.ds(KS * (NC + j) + k, 1)])
                ins.then_inc(s_labs, 1)

            def lane_step(j, b, n, more):
                if more(1):
                    lane_distance(j + 1, 1 - b)
                act.wait_ge(s_labs, j + 1)
                act.wait_ge(s_invmm, NC + j - 1)
                nc.scalar.activation(lane_oh[:, b, 0:KS_ACT, :], lane_abs[:, b, :, :], ACT.Relu, bias=1.0,
                                     scale=-1.0).then_inc(s_laneoh, 1)
            lane_distance(0, 0)
            ahead(act, STEPS - NC, lane_step)

            def copy_features(q):
                act.wait_ge(s_recT, q + 1)
                wait_if(act, s_hmm, q)
                nc.scalar.copy(fT[:], ps[:, 6, 0:128]).then_inc(s_fT, 1)

            def softplus_exp(q):
                act.wait_ge(s_hmm, q + 1)
                wait_if(act, s_h, q)
                nc.scalar.activation(sp_t[:, 0, :], ps[:, 7, :], ACT.Abs, bias=bf1[:, 0:1]).then_inc(s_act, 1)
                nc.scalar.activation(sp_t[:, 2, :], ps[:, 7, :], ACT.Relu, bias=bf1[:, 0:1]).then_inc(s_hread, 1)
                act.wait_ge(s_act, 2 * q + 1)
                nc.scalar.activation(sp_t[:, 1, :], sp_t[:, 0, :], ACT.Exp, scale=-1.0).then_inc(s_act, 1)

            def softplus_ln(q):
                act.wait_ge(s_act, 2 * q + 2)
                nc.scalar.activation(sp_t[:, 0, :], sp_t[:, 1, :], ACT.Ln, bias=1.0).then_inc(s_sp, 1)

            def scaled(q, m4, t):
                act.wait_ge(s_sc, HALF * q + t + 1)
                for i in range(3):
                    ins = nc.scalar.activation(msg[:, t, 5 + i, :], msg[:, t, 8, :], ACT.Copy,
                                               scale=rec[:, m4, t, R_U + i:R_U + i + 1])
                ins.then_inc(s_msga, 1)

            act.wait_ge(s_winf, 48)
            act.preload_act_table_set("natural_log_exp_and_others")
            copy_features(0)
            softplus_exp(0)
            softplus_ln(0)
            copy_features(1)

            def step(q, m4, n4, n2):
                scaled(q, m4, 0)
                scaled(q, m4, 1)
                softplus_exp(q + 1)
                softplus_ln(q + 1)
                scaled(q, m4, 2)
                copy_features(q + 2)
                scaled(q, m4, 3)
            halves(act, step)
            chain[0] = 2 * (HALVES + 1)

            def copy_aT(c, b):
                act.wait_ge(s_aggT, c + 1)
                wait_if(act, s_sv, c - 1)
                nc.scalar.copy(aT[:, b, 4:8, :], ps[:, 2 * b + 1, 0:4 * P].rearrange("p (m n) -> p m n", m=4)).then_inc(s_aTa, 1)

            def chunk(c, b, n, more):
                act.wait_ge(s_sv, c + 1)
                wait_if(act, s_spT, c)
                nc.scalar.activation(sT[:, 0, :], ps[:, 6 + b, 0:P], ACT.Abs).then_inc(s_act, 1)
                nc.scalar.activation(sT[:, 2, :], ps[:, 6 + b, 0:P], ACT.Relu)
                act.wait_ge(s_act, chain[0] + 2 * c + 1)
                nc.scalar.activation(sT[:, 1, :], sT[:, 0, :], ACT.Exp, scale=-1.0).then_inc(s_act, 1)
                act.wait_ge(s_act, chain[0] + 2 * c + 2)
                nc.scalar.activation(sT[:, 0, :], sT[:, 1, :], ACT.Ln, bias=1.0).then_inc(s_spa, 1)
                if more(2):
                    copy_aT(c + 2, b)
            copy_aT(0, 0)
            copy_aT(1, 1)
            ahead(act, NC, chunk)
            chain[0] += 2 * NC

            act.wait_ge(s_stats, 2)
            nc.scalar.activation(ln_t[:, 3, :], ln_t[:, 2, :], ACT.Sqrt).then_inc(s_sqrt, 1)
            act.preload_act_table_set("natural_log_exp_and_others")
            act.wait_ge(s_norm, 2)

            def norm_y(c, b, n):
                wait_if(act, s_ynT, c - 1)
                wait_if(act, s_yst[b], 16 * n)
                nc.scalar.activation(xn[:, b, :], x[:, bass.ds(c, 1), :].rearrange("p o d -> p (o d)"), ACT.Identity,
                                     bias=shift[:, bass.ds(c, 1)], scale=rstd[:, bass.ds(c, 1)]).then_inc(s_yn, 1)

            def norm(c, b, n, more):
                act.wait_ge(s_ynT, c + 1)
                wait_if(act, s_lgmm, c - 1)
                nc.scalar.copy(xT[:, b, :], ps[:, b, 0:4 * P]).then_inc(s_yT, 1)
                if more(2):
                    norm_y(c + 2, b, n + 1)
            norm_y(0, 0, 0)
            norm_y(1, 1, 0)
            ahead(act, NC, norm)

            act.wait_ge(s_gmax, 1)
            nc.scalar.activation(g[:, 1, :, :], g[:, 0, :, :], ACT.Exp).then_inc(s_gexp, 1)

            def expert(e, b, n):
                for a in range(2):
                    act.wait_ge(s_hid, 2 * e + a + 1)
                    if a == 0:
                        wait_if(act, s_eo, 3 * e)
                    nc.scalar.activation(hT[:, a, :], ps[:, 3 + a, 0:CAP], ACT.Relu).then_inc(s_hT, 1)
                wait_if(act, s_yost[b], 16 * n)
                for j in range(2):
                    act.wait_ge(s_eo, 3 * e + j + 1)
                    nc.scalar.copy(yo[:, b, j, :], ps[0:SP, 5 + j, :]).then_inc(s_yoa, 1)
            twos(act, NE, expert)

        @block.vector
        def _(dve):
            chain = [0]

            def link(ins):
                chain[0] += 1
                ins.then_inc(s_dve, 1)
                dve.wait_ge(s_dve, chain[0])

            v = nc.vector

            dve.wait_ge(s_pool_const, 3)
            v.tensor_scalar(thr[:], iota_i[0:P, 0:NC + 1], float(P), None, ALU.mult)
            v.memset(idx_all[:, TILES:SLOTCOLS], 0)
            v.memset(valid[:, TILES:SLOTCOLS], 0.0)
            v.memset(eidx[:, 3 * NE:3 * NE + 3], 0)
            link(v.tensor_copy(part_f[:], part_i[:]))
            link(v.tensor_copy(iota_f[:], iota_i[:]))
            edge_halves = edge_w[:].bitcast(BF16).rearrange("p (k w) -> p k w", w=2)
            v.tensor_scalar(slot_i[:, 0, :], edge_i[:], 127, None, ALU.bitwise_and)
            link(v.tensor_scalar(slot_i[:, 1, :], edge_i[:], 7, None, ALU.arith_shift_right))
            v.tensor_copy(edge_halves[:, :, 0], slot_i[:, 0, :])
            link(v.tensor_scalar(edge_halves[:, :, 1], slot_i[:, 1, :], 128.0, 128.0, ALU.mult, ALU.add))

            def norm_scales(which):
                me, mo = stats[:, :, 1], stats[:, :, 4]
                link(v.tensor_tensor(ln_t[:, 0, :], me, mo, ALU.add))
                link(v.tensor_tensor(ln_t[:, 1, :], me, mo, ALU.subtract))
                link(v.tensor_tensor(ln_t[:, 2, :], stats[:, :, 2], stats[:, :, 5], ALU.add))
                link(v.tensor_scalar(ln_t[:, 4, :], ln_t[:, 1, :], 0.5, None, ALU.mult))
                link(v.tensor_tensor(ln_t[:, 5, :], ln_t[:, 4, :], ln_t[:, 4, :], ALU.mult))
                link(v.tensor_scalar(ln_t[:, 4, :], ln_t[:, 2, :], 1.0 / D, EPS, ALU.mult, ALU.add))
                v.tensor_tensor(ln_t[:, 2, :], ln_t[:, 4, :], ln_t[:, 5, :], ALU.add).then_inc(s_stats, 1)

            def norm_finish(which):
                link(v.reciprocal(ln_t[:, 4, :], ln_t[:, 3, :]))
                link(v.tensor_tensor(ln_t[:, 5, :], ln_t[:, 2, :], ln_t[:, 4, :], ALU.mult))
                link(v.tensor_tensor(ln_t[:, 4, :], ln_t[:, 5, :], ln_t[:, 3, :], ALU.add))
                link(v.tensor_scalar(ln_t[:, 5, :], ln_t[:, 4, :], 0.5, None, ALU.mult))
                link(v.reciprocal(rstd[:], ln_t[:, 5, :]))
                v.scalar_tensor_tensor(shift[:], ln_t[:, 0, :], -0.5, rstd[:], ALU.mult, ALU.mult).then_inc(s_norm, 1)

            dve.wait_ge(s_srcin, 16)
            link(v.tensor_copy(srcf[:], src_i[:]))
            link(v.tensor_tensor(ge, srcf[:].unsqueeze(1).broadcast_to([P, NC + 1, EC]),
                                 thr[:].unsqueeze(2).broadcast_to([P, NC + 1, EC]), ALU.is_ge))
            link(v.tensor_tensor(ind, ge[:, 0:NC, :], ge[:, 1:NC + 1, :], ALU.subtract))
            v.tensor_reduce(cnt[:, 0, :], ind, AX.X, ALU.add).then_inc(s_rowtot, 1)

            dve.wait_ge(s_reset, 2)
            link(v.tensor_tensor_scan(incl_flat, bin_reset[:].rearrange("p b k -> p (b k)"), ind_flat, 0.0, ALU.mult, ALU.add))
            dve.wait_ge(s_cntmm, 1)
            link(v.tensor_scalar(cnt_i[:], ps[0:P, 0, 16:16 + NC], 255.0, None, ALU.add))
            link(v.tensor_scalar(cnt_i[:], cnt_i[:], 8, None, ALU.arith_shift_right))
            link(v.tensor_copy(cnt[:, 1, :], cnt_i[:]))
            link(v.memset(cnt[:, 6, :], 1.0))
            link(v.tensor_tensor_scan(cnt[:, 2, :], cnt[:, 6, :], cnt[:, 1, :], 0.0, ALU.mult, ALU.add))
            link(v.tensor_tensor(cnt[:, 3, :], cnt[:, 2, :], cnt[:, 1, :], ALU.subtract))
            link(v.tensor_scalar(cnt[:, 4, :], cnt[:, 3, :], 256.0, -1.0, ALU.mult, ALU.add))
            link(v.tensor_tensor(cnt[:, 5, :], cnt[:, 4, :], ps[0:P, 0, 0:NC], ALU.add))
            link(v.tensor_tensor(incl, incl, cnt[:, 5, :].unsqueeze(2).broadcast_to([P, NC, EC]), ALU.add))
            link(v.tensor_tensor(incl, incl, ind, ALU.mult))
            dve.wait_ge(s_xin, 16)
            with dve.Fori(0, NC) as c:
                v.bn_stats(stats[:, bass.ds(c, 1), :].rearrange("p o s -> p (o s)"),
                           x[:, bass.ds(c, 1), :].rearrange("p o d -> p (o d)")).then_inc(s_dve, 1)
            chain[0] += NC
            dve.wait_ge(s_dve, chain[0])
            norm_scales(0)
            dve.wait_ge(s_evin, 48)
            link(v.tensor_tensor(nrm[:, 1:4, :].rearrange("p i k -> p k i"), ev[:], ev[:], ALU.mult))
            v.tensor_reduce(nrm[:, 0, :], nrm[:, 1:4, :].rearrange("p i k -> p k i"), AX.X, ALU.add).then_inc(s_nrm2, 1)
            dve.wait_ge(s_sqrt, 1)
            norm_finish(0)

            link(v.tensor_reduce(chunkf[:], incl.rearrange("p b k -> p k b"), AX.X, ALU.add))
            link(v.tensor_copy(slot_i[:, 0, :], chunkf[:]))
            link(v.tensor_scalar(slot_i[:, 1, :], slot_i[:, 0, :], 7, None, ALU.arith_shift_right))
            link(v.tensor_scalar(slot_i[:, 2, :], slot_i[:, 0, :], 127, None, ALU.bitwise_and))
            link(v.tensor_copy(tile_f[:], slot_i[:, 1, :]))
            link(v.tensor_copy(lane_f[:], slot_i[:, 2, :]))
            v.tensor_scalar(lane_neg[:], lane_f[:], -1.0, None, ALU.mult).then_inc(s_lane, 1)

            def tile_step(s, b, n, lanes_from=KS_ACT):
                wait_if(dve, s_invmm, s - 1)
                for k in range(KS):
                    col = KS * s + k
                    if k >= lanes_from:
                        v.tensor_scalar(lane_oh[:, b, k, :], iota_f[0:P, 0:128], lane_f[:, bass.ds(col, 1)], None,
                                        ALU.is_equal)
                    ins = v.tensor_scalar(tile_oh[:, b, k, :], iota_f[0:P, 0:TILES], tile_f[:, bass.ds(col, 1)],
                                          edge_w[:, bass.ds(col, 1)], ALU.is_equal, ALU.mult)
                ins.then_inc(s_slotoh, 1)
            twos(dve, NC, lambda s, b, n: tile_step(s, b, n, 0))

            link(v.tensor_scalar(slot_i[:, 0, :], srcf[:], 1.0 / P, 0.5 / P, ALU.mult, ALU.add))
            link(v.tensor_copy(chunkf[:], slot_i[:, 0, :]))
            link(v.scalar_tensor_tensor(chunkf[:], chunkf[:], -float(P), srcf[:], ALU.mult, ALU.add))
            link(v.tensor_scalar(srcf[:], chunkf[:], 0.0, float(P), ALU.is_lt, ALU.mult))
            v.tensor_tensor(rec_all[:, :, R_SRC], srcf[:], chunkf[:], ALU.add)
            dve.wait_ge(s_sqrt, 2)
            link(v.reciprocal(nrm[:, 2, :], nrm[:, 1, :]))
            link(v.tensor_tensor(nrm[:, 3, :], nrm[:, 0, :], nrm[:, 2, :], ALU.mult))
            link(v.tensor_tensor(nrm[:, 2, :], nrm[:, 3, :], nrm[:, 1, :], ALU.add))
            link(v.tensor_scalar(nrm[:, 3, :], nrm[:, 2, :], 0.5, None, ALU.mult))
            v.reciprocal(nrm[:, 1, :], nrm[:, 3, :]).then_inc(s_unit, 1)

            with dve.Fori(NC // 2, STEPS // 2) as i:
                for b in range(2):
                    tile_step(2 * i + b, b, i)

            dve.wait_ge(s_invmm, STEPS)
            parts = ps[:, 1, 0:2 * TILES].rearrange("p (t w) -> p w t", w=2)
            v.tensor_scalar(valid[:, 0:TILES], parts[:, 1, :], 1.0, None, ALU.min)
            link(v.tensor_reduce(idx_f[:], ps[:, 1, 0:2 * TILES].rearrange("p (t w) -> p t w", w=2), AX.X, ALU.add))
            v.tensor_scalar(idx_all[:, 0:TILES], idx_f[:], -128.0, 0.0, ALU.add, ALU.max).then_inc(s_idx, 1)
            link(v.tensor_tensor(pair_ge[:], cnt[0:1, 2, :].unsqueeze(1).broadcast_to([1, PAIRS, NC]),
                                 iota_f[0:1, 0:PAIRS].unsqueeze(2).broadcast_to([1, PAIRS, NC]), ALU.is_le))
            link(v.tensor_reduce(pair_f[:, 0, :], pair_ge[:], AX.X, ALU.add))
            link(v.tensor_scalar(pair_chunk[:], pair_f[:, 0, :], float(NC - 1), None, ALU.min))

            def make_h(q, b):
                dve.wait_ge(s_sp, q + 1)
                wait_if(dve, s_w, HALF * (q - 1))
                v.scalar_tensor_tensor(h[:, b, :], sp_t[:, 2, :], -LN2, sp_t[:, 0, :], ALU.add, ALU.add).then_inc(s_h, 1)

            def messages(q, m4, n2, t):
                T = HALF * q + t
                slot = HALF * (m4 % 2) + t
                xs = xg[:, slot, :, :]
                u = rec[:, m4, t, :]
                W = ps[:, t % 2, :].rearrange("p (g c) -> p g c", g=4)
                m = msg[:, t, :, :]
                if t == 0:
                    dve.wait_ge(s_xgin[m4 % 2], 64 * (n2 + 1))
                v.tensor_scalar(dot[:, 0, :], xs[:, 1, :], u[:, R_U:R_U + 1], None, ALU.mult).then_inc(s_dot, 1)
                dve.wait_ge(s_w, T + 1)
                wait_if(dve, s_scat, T - 3)
                v.tensor_tensor(m[:, 0:9:8, :], W[:, 0:2, :], xs[:, 0:1, :].broadcast_to([128, 2, C]),
                                ALU.mult).then_inc(s_sc, 1)
                dve.wait_ge(s_dot, 2 * T + 1)
                v.scalar_tensor_tensor(dot[:, 1, :], xs[:, 2, :], u[:, R_U + 1:R_U + 2], dot[:, 0, :],
                                       ALU.mult, ALU.add).then_inc(s_dot, 1)
                v.tensor_tensor(m[:, 1:4, :], W[:, 3:4, :].broadcast_to([128, 3, C]), xs[:, 1:4, :], ALU.mult)
                dve.wait_ge(s_dot, 2 * T + 2)
                link3 = v.scalar_tensor_tensor(dot[:, 2, :], xs[:, 3, :], u[:, R_U + 2:R_U + 3], dot[:, 1, :],
                                               ALU.mult, ALU.add)
                link3.then_inc(s_dot3, 1)
                dve.wait_ge(s_dot3, T + 1)
                v.tensor_tensor(m[:, 4, :], W[:, 2, :], dot[:, 2, :], ALU.mult).then_inc(s_msgv, 1)

            def accumulate(j, b):
                chunk = dve.value_load(pair_chunk[0:1, bass.ds(j, 1)], min_val=0, max_val=NC - 1)
                dve.wait_ge(s_scat, 2 * j + 2)
                wait_if(dve, s_acc, j)
                to = agg[:, bass.ds(chunk, 1), :].rearrange("p o m -> p (o m)")
                v.tensor_tensor(to, to, ps[0:P, 2 + 2 * b:4 + 2 * b, :].rearrange("p a m -> p (a m)"),
                                ALU.add).then_inc(s_acc, 1)

            def one_hot(q, m4, t):
                slot = HALF * (m4 % 2) + t
                if t == 0:
                    dve.wait_ge(s_rv, q + 1)
                wait_if(dve, s_scat, HALF * (q - 2) + t + 1)
                v.tensor_scalar(onehot[:, slot, :], iota_f[:, 0:P], rec[:, m4, t, R_SRC:R_SRC + 1],
                                rv[:, m4 % 2, t:t + 1], ALU.is_equal, ALU.mult).then_inc(s_onehot, 1)

            for t in range(HALF):
                one_hot(0, 0, t)
            make_h(0, 0)

            def step(q, m4, n4, n2):
                after = (m4 + 1) % 4
                messages(q, m4, n2, 0)
                one_hot(q + 1, after, 0)
                messages(q, m4, n2, 1)
                one_hot(q + 1, after, 1)
                if not (isinstance(q, int) and q == 0):
                    accumulate(2 * q - 1, 1)
                messages(q, m4, n2, 2)
                one_hot(q + 1, after, 2)
                make_h(q + 1, after % 2)
                messages(q, m4, n2, 3)
                one_hot(q + 1, after, 3)
                accumulate(2 * q, 0)
            halves(dve, step)
            accumulate(PAIRS - 1, 1)

            def copy_aT(c, b):
                dve.wait_ge(s_aggT, c + 1)
                wait_if(dve, s_sv, c - 1)
                v.tensor_copy(aT[:, b, 0:4, :], ps[:, 2 * b, 0:4 * P].rearrange("p (m n) -> p m n", m=4)).then_inc(s_aTv, 1)

            def chunk(c, b, n, more):
                dve.wait_ge(s_sv, c + 1)
                wait_if(dve, s_o, c - 1)
                v.tensor_copy(vT[:, b, :, :], ps[:, 4 + b, P:4 * P].rearrange("p (i n) -> p i n", i=3)).then_inc(s_vT, 1)
                if more(2):
                    copy_aT(c + 2, b)
                dve.wait_ge(s_spa, c + 1)
                v.scalar_tensor_tensor(spT[:, b, :], sT[:, 2, :], -LN2, sT[:, 0, :], ALU.add, ALU.add).then_inc(s_spT, 1)
                dve.wait_ge(s_o, c + 1)
                xc = x[:, bass.ds(c, 1), :].rearrange("p o d -> p (o d)")
                v.tensor_tensor(xc[:, 0:C], xc[:, 0:C], ps[0:P, 6 + b, 0:C], ALU.add)
                xv = xc[:, C:D].rearrange("p (d i) -> p i d", i=3)
                v.tensor_tensor(xv, xv, ps[0:P, 6 + b, C:D].rearrange("p (i d) -> p i d", i=3), ALU.add).then_inc(s_x1, 1)
                dve.wait_ge(s_x1, c + 1)
                v.bn_stats(stats[:, bass.ds(c, 1), :].rearrange("p o s -> p (o s)"), xc).then_inc(s_dve, 1)
            copy_aT(0, 0)
            copy_aT(1, 1)
            ahead(dve, NC, chunk)
            chain[0] += NC
            dve.wait_ge(s_dve, chain[0])
            norm_scales(1)
            dve.wait_ge(s_sqrt, 3)
            norm_finish(1)

            def logits(c, b, n):
                dve.wait_ge(s_lgmm, c + 1)
                v.tensor_copy(g[:, 2, bass.ds(c, 1), :].rearrange("p o e -> p (o e)"), ps[0:P, 2 + b, 0:NE]).then_inc(s_lg, 1)
            twos(dve, NC, logits)
            dve.wait_ge(s_lg, NC)

            def by_expert(a):
                return a.unsqueeze(2).broadcast_to([P, NC, NE])
            iota_e = iota_f[0:P, 0:NE].unsqueeze(1).broadcast_to([P, NC, NE])
            link(v.tensor_reduce(gs[:, 0, :], g[:, 2, :, :], AX.X, ALU.max))
            link(v.tensor_tensor(g[:, 0, :, :], g[:, 2, :, :], by_expert(gs[:, 0, :]), ALU.subtract))
            v.engine_nop().then_inc(s_gmax, 1)
            dve.wait_ge(s_gexp, 1)
            link(v.tensor_reduce(gs[:, 0, :], g[:, 1, :, :], AX.X, ALU.add))
            link(v.reciprocal(gs[:, 1, :], gs[:, 0, :]))
            link(v.tensor_tensor(g[:, 0, :, :], g[:, 1, :, :], by_expert(gs[:, 1, :]), ALU.mult))
            for a in range(2):
                raw = g[:, 0, :, :]
                link(v.tensor_reduce(gs[:, 2 + a, :], raw, AX.X, ALU.max))
                link(v.tensor_tensor(g[:, 1, :, :], raw, by_expert(gs[:, 2 + a, :]), ALU.is_equal))
                link(v.tensor_scalar(g[:, 2, :, :], g[:, 1, :, :], -float(NE), float(NE), ALU.mult, ALU.add))
                link(v.tensor_tensor(g[:, 1, :, :], g[:, 2, :, :], iota_e, ALU.add))
                link(v.tensor_reduce(gs[:, 4 + a, :], g[:, 1, :, :], AX.X, ALU.min))
                link(v.tensor_tensor(g[:, 4 + a, :, :], iota_e, by_expert(gs[:, 4 + a, :]), ALU.is_equal))
                if a == 0:
                    link(v.tensor_tensor(g[:, 1, :, :], raw, g[:, 4, :, :], ALU.mult))
                    link(v.tensor_tensor(raw, raw, g[:, 1, :, :], ALU.subtract))
            v.engine_nop().then_inc(s_masks, 1)
            link(v.tensor_tensor(gs[:, 6, :], gs[:, 2, :], gs[:, 3, :], ALU.add))
            link(v.tensor_scalar(gs[:, 6, :], gs[:, 6, :], 1e-9, None, ALU.add))
            link(v.reciprocal(gs[:, 7, :], gs[:, 6, :]))
            link(v.tensor_tensor(gs[:, 2:4, :], gs[:, 2:4, :], gs[:, 7:8, :].broadcast_to([P, 2, NC]), ALU.mult))

            link(v.memset(reset[:], 1.0))
            link(v.memset(reset[:, :, 0:1], 0.0))
            dve.wait_ge(s_cum, 1)
            for a in range(2):
                tot = ps[0:P, 5, 160 * a:160 * a + 160].rearrange("p (c e) -> p e c", c=NC)
                link(v.tensor_copy(totT[:, a, :, :], tot))
                link(v.tensor_tensor_scan(preT[:, a, :, :].rearrange("p e c -> p (e c)"),
                                          reset[:].rearrange("p e c -> p (e c)"),
                                          totT[:, a, :, :].rearrange("p e c -> p (e c)"), 0.0, ALU.mult, ALU.add))
            link(v.tensor_tensor(totT[:], preT[:], totT[:], ALU.subtract))
            link(v.tensor_scalar(reset[:, :, 0:1], preT[:, 0, :, NC - 1:NC], float(CAP), None, ALU.min))
            link(v.tensor_tensor(totT[:, 1, :, :], totT[:, 1, :, :], reset[:, :, 0:1].broadcast_to([P, NE, NC]), ALU.add))
            for a in range(2):
                cum = ps[0:P, 4, 160 * a:160 * a + 160].rearrange("p (c e) -> p c e", c=NC)
                link(v.tensor_tensor(g[:, 6 + a, :, :], cum, totT[:, a, :, :].rearrange("p e c -> p c e"), ALU.add))
                link(v.tensor_tensor(g[:, 8 + a, :, :], g[:, 6 + a, :, :], g[:, 4 + a, :, :], ALU.mult))
                link(v.tensor_reduce(gs[:, 8 + a, :], g[:, 8 + a, :, :], AX.X, ALU.add))
            pos, fits, gate, expert_id = gs[:, 8:10, :], gs[:, 10:12, :], gs[:, 2:4, :], gs[:, 4:6, :]
            link(v.tensor_scalar(fits, pos, float(CAP), None, ALU.is_lt))
            link(v.tensor_tensor(gate, gate, fits, ALU.mult))
            link(v.scalar_tensor_tensor(gs[:, 12:14, :], expert_id, float(CAP), pos, ALU.mult, ALU.add))
            link(v.tensor_tensor(cslot[:], gs[:, 12:14, :], fits, ALU.mult))
            link(v.tensor_scalar(gs[:, 12:14, :], pos, float(SP), None, ALU.is_ge))
            link(v.tensor_scalar(gs[:, 14:16, :], pos, float(2 * SP), None, ALU.is_ge))
            link(v.tensor_tensor(gs[:, 12:14, :], gs[:, 12:14, :], gs[:, 14:16, :], ALU.add))
            link(v.scalar_tensor_tensor(etile[:], expert_id, float(SJ), gs[:, 12:14, :], ALU.mult, ALU.add))
            link(v.scalar_tensor_tensor(gs[:, 14:16, :], gs[:, 12:14, :], -float(SP), pos, ALU.mult, ALU.add))
            link(v.scalar_tensor_tensor(gs[:, 12:14, :], gs[:, 14:16, :], 1.0, fits, ALU.add, ALU.mult))
            link(v.tensor_scalar(elane[:], gs[:, 12:14, :], -1.0, None, ALU.add))
            link(v.tensor_scalar(cp1[:], iota_f[0:P, 0:NC], 1.0, None, ALU.add))
            for a in range(2):
                link(v.tensor_tensor(elane_oh[:, a, :, :], iota_f[0:P, 0:SP].unsqueeze(1).broadcast_to([P, NC, SP]),
                                     elane[:, a, :].unsqueeze(2).broadcast_to([P, NC, SP]), ALU.is_equal))
                link(v.tensor_tensor(etile_eq[:, a, :, :], iota_f[0:P, 0:3 * NE].unsqueeze(1).broadcast_to([P, NC, 3 * NE]),
                                     etile[:, a, :].unsqueeze(2).broadcast_to([P, NC, 3 * NE]), ALU.is_equal))
                link(v.tensor_tensor(etile_oh[:, a, :, 0, :], etile_eq[:, a, :, :],
                                     cp1[:].unsqueeze(2).broadcast_to([P, NC, 3 * NE]), ALU.mult))
                link(v.tensor_scalar(etile_oh[:, a, :, 1, :], etile_eq[:, a, :, :], part_f[0:P, 0:1], None, ALU.mult))
            v.engine_nop().then_inc(s_eoh, 1)
            dve.wait_ge(s_einv, 1)
            link(v.tensor_scalar(eidx_f[:, 0, :], ps[0:SP, 6, 0:3 * NE], float(P), -float(P), ALU.mult, ALU.add))
            link(v.tensor_tensor(eidx_f[:, 1, :], eidx_f[:, 0, :], ps[0:SP, 6, 3 * NE:6 * NE], ALU.add))
            v.tensor_scalar(eidx[:, 0:3 * NE], eidx_f[:, 1, :], 0.0, None, ALU.max).then_inc(s_eidx, 1)

            def copy_xd(e, b, n):
                wait_if(dve, s_hid, 2 * e)
                for j in range(SJ):
                    dve.wait_ge(s_xdT, SJ * e + j + 1)
                    v.tensor_copy(xdT[:, :, SP * j:SP * j + SP],
                                  ps[:, j, 0:4 * SP].rearrange("p (a n) -> p a n", a=4)).then_inc(s_xdTsb, 1)

            def expert(e, b, n):
                copy_xd(e + 1, 1 - b, n)
                wait_if(dve, s_yost[b], 16 * n)
                dve.wait_ge(s_eo, 3 * e + 3)
                v.tensor_copy(yo[:, b, 2, :], ps[0:SP, 7, :]).then_inc(s_yov, 1)
            copy_xd(0, 0, 0)
            twos(dve, NE, expert)

            for c in range(NC):
                dve.wait_ge(s_ygin[c % RING], 32 * (c // RING + 1))
                link(v.scalar_tensor_tensor(x[:, c, :], yg[:, c % RING, 0, :], gs[:, 2, c:c + 1], x[:, c, :],
                                            ALU.mult, ALU.add))
                v.scalar_tensor_tensor(x[:, c, :], yg[:, c % RING, 1, :], gs[:, 3, c:c + 1], x[:, c, :],
                                       ALU.mult, ALU.add).then_inc(s_out, 1)

        @block.tensor
        def _(pe):
            mm = nc.tensor.matmul
            pe.wait_ge(s_pool_const, 9)

            pe.wait_ge(s_rowtot, 1)
            mm(ps[0:P, 0, 0:NC], tri[:], cnt[:, 0, :], start=True, stop=True)
            mm(ps[0:P, 0, 16:16 + NC], ones[:], cnt[:, 0, :], start=True, stop=True).then_inc(s_cntmm, 1)

            pe.wait_ge(s_winf, 48)

            def transposes_of_xn(b, bank, signal):
                for m in range(4):
                    part = xn[:, b, 0:C] if m == 0 else xn[:, b, C + m - 1:D:3]
                    ins = nc.tensor.transpose(ps[:, bank, P * m:P * m + P], part, ident[0:P, 0:P])
                ins.then_inc(signal, 1)

            def xn_T(c, b):
                pe.wait_ge(s_xn, c + 1)
                wait_if(pe, s_xT, c - 1)
                transposes_of_xn(b, 6 + b, s_xnT)

            def invert(s, b, lanes_of_act=True):
                pe.wait_ge(s_slotoh, s + 1)
                if lanes_of_act:
                    pe.wait_ge(s_laneoh, s - NC + 1)
                for k in range(KS):
                    first, last = isinstance(s, int) and s == k == 0, isinstance(s, int) and s == STEPS - 1 and k == KS - 1
                    ins = mm(ps[:, 1, 0:2 * TILES], lane_oh[:, b, k, :], tile_oh[:, b, k, :].bitcast(BF16),
                             start=first, stop=last)
                ins.then_inc(s_invmm, 1)

            def project(c, b, n, more):
                if more(1):
                    xn_T(c + 1, 1 - b)
                pe.wait_ge(s_xT, c + 1)
                wait_if(pe, s_tabsb, c - 1)
                for m in range(4):
                    ins = mm(ps[0:P, 4 + b, C * m:C * m + C], xT[:, b, P * m:P * m + P],
                             (win_s_sb if m == 0 else win_v_sb)[:], start=True, stop=True)
                ins.then_inc(s_tabmm, 1)
                invert(c, b, False)
            xn_T(0, 0)
            ahead(pe, NC, project)

            with pe.Fori(NC // 2, STEPS // 2 - 1) as i:
                for b in range(2):
                    invert(2 * i + b, b)
            invert(STEPS - 2, 0)
            invert(STEPS - 1, 1)

            def records(q, m4, n4):
                pe.wait_ge(s_recin[m4], 64 * (n4 + 1))
                wait_if(pe, s_fT, q)
                nc.tensor.transpose(ps[:, 6, 0:128], rec[:, m4, :, :].rearrange("p t r -> p (t r)"),
                                    ident[:]).then_inc(s_recT, 1)

            def hidden(q):
                pe.wait_ge(s_fT, q + 1)
                wait_if(pe, s_hread, q)
                for t in range(HALF):
                    ins = mm(ps[:, 7, 128 * t:128 * t + 128], wf1[:, t, :], fT[:], start=True, stop=True)
                ins.then_inc(s_hmm, 1)

            def filters(q, b, t):
                if t == 0:
                    pe.wait_ge(s_h, q + 1)
                wait_if(pe, s_msgv, HALF * q + t - 1)
                mm(ps[:, t % 2, :], h[:, b, 128 * t:128 * t + 128], wf2[:].rearrange("p g c -> p (g c)"),
                   start=True, stop=False)
                mm(ps[:, t % 2, :], ones3[:], bf2_split[:].rearrange("p g c -> p (g c)"),
                   start=False, stop=True).then_inc(s_w, 1)

            def sum_edges(q, m4, t):
                T = HALF * q + t
                pe.wait_ge(s_onehot, T + 1)
                pe.wait_ge(s_msgv, T + 1)
                pe.wait_ge(s_msga, T + 1)
                pair = t // 2
                if t % 2 == 0:
                    wait_if(pe, s_acc, 2 * q + pair - 1)
                for half in range(2):
                    ins = mm(ps[0:P, 2 + 2 * pair + half, :], onehot[:, HALF * (m4 % 2) + t, :],
                             msg[:, t, 4 * half:4 * half + 4, :].rearrange("p m c -> p (m c)"),
                             start=t % 2 == 0, stop=t % 2 == 1)
                ins.then_inc(s_scat, 1)

            pe.wait_ge(s_tabsb, NC)
            pe.wait_ge(s_wprep, 1)
            pe.wait_ge(s_wf1in, 64)
            records(0, 0, 0)
            hidden(0)
            records(1, 1, 0)
            filters(0, 0, 0)
            filters(0, 0, 1)

            def step(q, m4, n4, n2):
                b = m4 % 2
                hidden(q + 1)
                filters(q, b, 2)
                sum_edges(q, m4, 0)
                filters(q, b, 3)
                sum_edges(q, m4, 1)
                filters(q + 1, 1 - b, 0)
                sum_edges(q, m4, 2)
                records(q + 2, (m4 + 2) % 4, n4 + (m4 + 2) // 4)
                filters(q + 1, 1 - b, 1)
                sum_edges(q, m4, 3)
            halves(pe, step)

            pe.wait_ge(s_acc, PAIRS)

            def sums_T(c, b, sums):
                wait_if(pe, s_aggc, c - 1)
                wait_if(pe, s_aTv, c - 1)
                wait_if(pe, s_aTa, c - 1)
                for m in range(8):
                    ins = nc.tensor.transpose(ps[:, 2 * b + m // 4, P * (m % 4):P * (m % 4) + P],
                                              sums[:, C * m:C * (m + 1)], ident[0:P, 0:P])
                ins.then_inc(s_aggT, 1)

            def products(c, b):
                pe.wait_ge(s_aTv, c + 1)
                pe.wait_ge(s_aTa, c + 1)
                wait_if(pe, s_x1, c - 1)
                wait_if(pe, s_vT, c - 1)
                mm(ps[:, 6 + b, 0:P], w1[:, 0, 0, :], aT[:, b, 0, :], start=True, stop=False)
                mm(ps[:, 6 + b, 0:P], w1[:, 0, 1, :], aT[:, b, 4, :], start=False, stop=True)
                mm(ps[:, 4 + b, P:4 * P], w1[:, 1, 0, :], aT[:, b, 5:8, :].rearrange("p m n -> p (m n)"),
                   start=True, stop=False)
                mm(ps[:, 4 + b, P:4 * P], w1[:, 1, 1, :], aT[:, b, 1:4, :].rearrange("p m n -> p (m n)"),
                   start=False, stop=True).then_inc(s_sv, 1)

            def outputs(c, b):
                pe.wait_ge(s_spT, c + 1)
                pe.wait_ge(s_vT, c + 1)
                mm(ps[0:P, 6 + b, 0:C], spT[:, b, :], w2[:, 0, :], start=True, stop=True)
                for i in range(3):
                    ins = mm(ps[0:P, 6 + b, C * (i + 1):C * (i + 2)], vT[:, b, i, :], w2[:, 1, :], start=True, stop=True)
                ins.then_inc(s_o, 1)

            def chunk(c, b, n, more):
                if more(2):
                    sums_T(c + 2, b, aggc[:, b, :])
                if more(1):
                    products(c + 1, 1 - b)
                outputs(c, b)
            sums_T(0, 0, agg[:, 0, :])
            sums_T(1, 1, agg[:, 1, :])
            products(0, 0)
            ahead(pe, NC, chunk)

            def yn_T(c, b):
                pe.wait_ge(s_yn, c + 1)
                wait_if(pe, s_yT, c - 1)
                for m in range(4):
                    ins = nc.tensor.transpose(ps[:, b, P * m:P * m + P], xn[:, b, C * m:C * m + C], ident[0:P, 0:P])
                ins.then_inc(s_ynT, 1)

            def logits(c, b, n, more):
                if more(1):
                    yn_T(c + 1, 1 - b)
                pe.wait_ge(s_yT, c + 1)
                wait_if(pe, s_lg, c - 1)
                for m in range(4):
                    ins = mm(ps[0:P, 2 + b, 0:NE], xT[:, b, P * m:P * m + P], wg[:, m, :], start=m == 0, stop=m == 3)
                ins.then_inc(s_lgmm, 1)
            yn_T(0, 0)
            ahead(pe, NC, logits)

            pe.wait_ge(s_masks, 1)
            masks = g[:, 4:6, :, :].rearrange("p a c e -> p (a c e)")
            mm(ps[0:P, 4, 0:320], tri[:], masks, start=True, stop=True)
            mm(ps[0:P, 5, 0:320], ones[:], masks, start=True, stop=True).then_inc(s_cum, 1)
            pe.wait_ge(s_eoh, 1)
            for a in range(2):
                for c in range(NC):
                    ins = mm(ps[0:SP, 6, 0:6 * NE], elane_oh[:, a, c, :],
                             etile_oh[:, a, c, :, :].rearrange("p w t -> p (w t)"),
                             start=a == 0 and c == 0, stop=a == 1 and c == NC - 1)
            ins.then_inc(s_einv, 1)

            def tokens_T(e, b, n):
                pe.wait_ge(s_xdin[b], 48 * (n + 1))
                for j in range(SJ):
                    wait_if(pe, s_xdTsb, SJ * (e - 1) + j + 1)
                    for m in range(4):
                        ins = nc.tensor.transpose(ps[:, j, SP * m:SP * m + SP], xd[:, b, j, C * m:C * m + C],
                                                  ident[0:SP, 0:SP])
                    ins.then_inc(s_xdT, 1)
            pe.wait_ge(s_eidx, 1)
            tokens_T(0, 0, 0)

            def expert(e, b, n):
                pe.wait_ge(s_we[b], 32 * (n + 1))
                pe.wait_ge(s_xdTsb, SJ * e + SJ)
                for a in range(2):
                    wait_if(pe, s_hT, 2 * (e - 1) + a + 1)
                    for m in range(4):
                        ins = mm(ps[:, 3 + a, 0:CAP], we1[:, b, m, 128 * a:128 * a + 128], xdT[:, m, :],
                                 start=m == 0, stop=m == 3)
                    ins.then_inc(s_hid, 1)
                tokens_T(e + 1, 1 - b, n + b)
                pe.wait_ge(s_hT, 2 * e + 2)
                for j in range(SJ):
                    if j < 2:
                        wait_if(pe, s_yoa, 2 * (e - 1) + j + 1)
                    else:
                        wait_if(pe, s_yov, e)
                    for a in range(2):
                        ins = mm(ps[0:SP, 5 + j, :], hT[:, a, SP * j:SP * j + SP], we2[:, b, a, :],
                                 start=a == 0, stop=a == 1)
                    ins.then_inc(s_eo, 1)
            twos(pe, NE, expert)


_INS = ["x", "src", "dst", "edge_attr_20", "edge_attr_3", "edge_weight", "L0_gnn_W_in2f_s", "L0_gnn_W_in2f_v",
        "L0_gnn_Wf1", "L0_gnn_bf1", "L0_gnn_Wf2", "L0_gnn_bf2", "L0_gnn_W1_s", "L0_gnn_W1_v", "L0_gnn_W2_s",
        "L0_gnn_W2_v", "L0_ffn_w_gating", "L0_ffn_w1", "L0_ffn_w2"]


def kernel(**inputs):
    import numpy as _np
    import concourse.bacc as _bacc
    from concourse import mybir as _mybir
    from concourse.bass_utils import run_bass_kernel_spmd as _run

    nc = _bacc.Bacc("TRN2", target_bir_lowering=False, num_devices=1)
    arrays, args = {}, []
    for name in _INS:
        a = _np.ascontiguousarray(inputs[name])
        arrays[f"in_{name}_dram"] = a
        args.append(nc.dram_tensor(f"in_{name}_dram", a.shape, _mybir.dt.from_np(a.dtype), kind="ExternalInput").ap())
    out = nc.dram_tensor("out_dram", (N, D), F32, kind="ExternalOutput").ap()
    build(nc, *args, out)
    r = _run(nc, [arrays], core_ids=[0])
    return r.results[0]["out_dram"]
```
